# Optimizing a Trainium2 kernel written in Bass

```python
import numpy as np
import jax
import jax.numpy as jnp

def _softmax(x, axis=-1):
    return jax.nn.softmax(x, axis=axis)

def _gelu(x):
    return jax.nn.gelu(x, approximate=True)

def _silu(x):
    return jax.nn.silu(x)

def _sigmoid(x):
    return jax.nn.sigmoid(x)

def _layernorm(x, axis=-1, eps=1e-05):
    m = jnp.mean(x, axis=axis, keepdims=True)
    v = jnp.var(x, axis=axis, keepdims=True)
    return (x - m) / jnp.sqrt(v + eps)

def _scatter_add(tgt, idx, src, axis=0):
    return tgt.at[idx].add(src)

def _segment_sum(src, seg, n):
    return jax.ops.segment_sum(src, seg, n)
kernel_name = 'mk_xattn_ffn_d2_seqx_r8_89bffc'

def setup_inputs(seed: int=0):
    np.random.seed(seed)
    _w = jnp.asarray

    def _rec_inputs():
        import jax
        import jax.numpy as jnp
        _rk = jax.random.key(seed)
        x = 7.22e-05 + 1 * jax.random.normal(jax.random.fold_in(_rk, 1), (16, 128, 256), jnp.float32)
        _lenS = 128 - jax.random.randint(jax.random.fold_in(_rk, 7), (16,), 0, max(1, 128 // 4) + 1, jnp.int32)
        _lenS2 = 128 - jax.random.randint(jax.random.fold_in(_rk, 8), (16,), 0, max(1, 128 // 4) + 1, jnp.int32)
        _ctx_2048P = jax.random.normal(jax.random.fold_in(_rk, 11), (16, 16, 256), jnp.float32)
        _ctx_2048c = jax.random.dirichlet(jax.random.fold_in(_rk, 511), 0.3 * jnp.ones((16,), jnp.float32), (16, 128))
        _ctx_2048t = jnp.einsum('bsk,bkd->bsd', _ctx_2048c, _ctx_2048P)
        _ctx_2048t = _ctx_2048t * jax.lax.rsqrt(jnp.mean(jnp.square(_ctx_2048t)) + 1e-12) * 0.953939
        ctx_2048 = 4.13588e-05 + 0.999923 * (_ctx_2048t + 0.3 * jax.random.normal(jax.random.fold_in(_rk, 611), (16, 128, 256), jnp.float32))
        _validS = jnp.arange(128)[None, :] < _lenS[:, None]
        _validS2 = jnp.arange(128)[None, :] < _lenS2[:, None]
        _causal = jnp.tril(jnp.ones((128, 128), dtype=bool))
        mask_BxS2_bk0 = jnp.logical_not(jnp.broadcast_to(_validS2[:, :], (16, 128)))
        return (x, ctx_2048, mask_BxS2_bk0)
    x, ctx_2048, mask_BxS2_bk0 = _rec_inputs()

    def _L0_xattn_setup():
        import jax, jax.numpy as jnp
        import numpy as np
        N_HEAD = 8
        key = jax.random.key(seed)
        k1, k2, k3 = jax.random.split(key, 3)
        b, d, m = (4, 128, 256)
        c, n = (128, 256)
        q = jax.random.normal(k1, (b, d, m), dtype=jnp.float32)
        k = jax.random.normal(k2, (d // d * b, d, n), dtype=jnp.float32).reshape(b, d, n)
        v = jax.random.normal(k3, (b, c, n), dtype=jnp.float32)
        return {'q': q, 'k': k, 'v': v}
    _L0_xattn_all = _L0_xattn_setup()
    _L0_xattn_in = {k: v for k, v in _L0_xattn_all.items() if k in ()}
    del _L0_xattn_all

    def _L0_ffn_setup():
        import jax, jax.numpy as jnp
        import numpy as np
        NUM_EXPERTS = 16
        C = 1.0
        key = jax.random.key(seed)
        k1, k2, k3 = jax.random.split(key, 3)
        b, s, h = (4, 256, 256)
        return {'x': jax.random.normal(k1, (b, s, h), dtype=jnp.float32), 'router_w': jax.random.normal(k2, (h, NUM_EXPERTS), dtype=jnp.float32) * 0.02, 'router_b': jnp.zeros((NUM_EXPERTS,), dtype=jnp.float32), 'expert_w': jax.random.normal(k3, (h, h), dtype=jnp.float32) * 0.02, 'expert_b': jnp.zeros((h,), dtype=jnp.float32)}
    _L0_ffn_all = _L0_ffn_setup()
    _L0_ffn_in = {k: v for k, v in _L0_ffn_all.items() if k in ('router_w', 'router_b', 'expert_w', 'expert_b')}
    del _L0_ffn_all

    def _L1_xattn_setup():
        import jax, jax.numpy as jnp
        import numpy as np
        key = jax.random.key(seed)
        k1, k2, k3 = jax.random.split(key, 3)
        B, S, D, M = (8, 256, 256, 128)
        hidden_states = jax.random.normal(k1, (B, S, D), dtype=jnp.float32)
        memory_tokens = jax.random.normal(k2, (B, M, D), dtype=jnp.float32)
        memory_mask = jax.random.randint(k3, (B, M), 0, 2).astype(jnp.bool_)
        return {'hidden_states': hidden_states, 'memory_tokens': memory_tokens, 'memory_mask': memory_mask}
    _L1_xattn_all = _L1_xattn_setup()
    _L1_xattn_in = {k: v for k, v in _L1_xattn_all.items() if k in ()}
    del _L1_xattn_all

    def _L1_ffn_setup():
        import jax, jax.numpy as jnp
        import numpy as np
        B, L, D = (4, 512, 256)
        DF = 4 * D
        CAPACITY_RATIO = 0.5
        key = jax.random.key(seed)
        ks = jax.random.split(key, 4)
        s = 0.02
        return {'x': jax.random.normal(ks[0], (B, L, D), dtype=jnp.float32), 'w_r': jax.random.normal(ks[1], (D,), dtype=jnp.float32) * s, 'b_r': jnp.zeros((), dtype=jnp.float32), 'w1': jax.random.normal(ks[2], (D, DF), dtype=jnp.float32) * s, 'b1': jnp.zeros((DF,), dtype=jnp.float32), 'w2': jax.random.normal(ks[3], (DF, D), dtype=jnp.float32) * s, 'b2': jnp.zeros((D,), dtype=jnp.float32)}
    _L1_ffn_all = _L1_ffn_setup()
    _L1_ffn_in = {k: v for k, v in _L1_ffn_all.items() if k in ('w_r', 'b_r', 'w1', 'b1', 'w2', 'b2')}
    del _L1_ffn_all
    return {'x': x, 'ctx_2048': ctx_2048, 'mask_BxS2_bk0': mask_BxS2_bk0, 'L0_ffn_router_w': _L0_ffn_in['router_w'], 'L0_ffn_router_b': _L0_ffn_in['router_b'], 'L0_ffn_expert_w': _L0_ffn_in['expert_w'], 'L0_ffn_expert_b': _L0_ffn_in['expert_b'], 'L1_ffn_w_r': _L1_ffn_in['w_r'], 'L1_ffn_b_r': _L1_ffn_in['b_r'], 'L1_ffn_w1': _L1_ffn_in['w1'], 'L1_ffn_b1': _L1_ffn_in['b1'], 'L1_ffn_w2': _L1_ffn_in['w2'], 'L1_ffn_b2': _L1_ffn_in['b2']}

def reference(x, ctx_2048, mask_BxS2_bk0, L0_ffn_router_w, L0_ffn_router_b, L0_ffn_expert_w, L0_ffn_expert_b, L1_ffn_w_r, L1_ffn_b_r, L1_ffn_w1, L1_ffn_b1, L1_ffn_w2, L1_ffn_b2):
    import jax
    import jax.numpy as jnp

    def _L0_xattn_ref(q, k, v):
        import jax, jax.numpy as jnp
        import numpy as np
        N_HEAD = 8
        b, d, m = q.shape
        c = v.shape[1]
        h = N_HEAD
        qh = q.reshape(b * h, d // h, m)
        kh = k.reshape(b * h, d // h, -1)
        vh = v.reshape(b * h, c // h, -1)
        scale = 1.0 / jnp.sqrt(jnp.asarray(d // h, dtype=q.dtype))
        qk = jnp.einsum('bdm,bdn->bmn', qh, kh) * scale
        sm = jax.nn.softmax(qk, axis=-1)
        ret = jnp.einsum('bmn,bcn->bcm', sm, vh)
        return ret.reshape(b, c, m)

    def _L0_ffn_ref(x, router_w, router_b, expert_w, expert_b):
        import jax, jax.numpy as jnp
        import numpy as np
        NUM_EXPERTS = 16
        C = 1.0
        b, s, h = x.shape
        bs = b * s
        k = min(int(bs * C / NUM_EXPERTS), bs)
        xf = x.reshape(bs, h)
        logits = xf @ router_w + router_b
        S = jax.nn.softmax(logits, axis=-1)
        G, idx = jax.lax.top_k(S.T, k)
        tokens = xf[idx]
        out = jnp.einsum('ekh,hd->ekd', tokens, expert_w) + expert_b
        weighted = G[..., None] * out
        y = jnp.zeros((bs, h), dtype=x.dtype).at[idx.reshape(-1)].add(weighted.reshape(-1, h))
        return y.reshape(b, s, h)

    def _L1_xattn_ref(hidden_states, memory_tokens, memory_mask):
        import jax, jax.numpy as jnp
        import numpy as np
        B, S, D = hidden_states.shape
        scale = 1.0 / jnp.sqrt(jnp.asarray(D, hidden_states.dtype))
        scores = jnp.einsum('bsd,bmd->bsm', hidden_states, memory_tokens) * scale
        neg_inf = jnp.asarray(-1e+30, scores.dtype)
        scores = jnp.where(memory_mask[:, None, :], scores, neg_inf)
        attn = jax.nn.softmax(scores, axis=-1)
        readout = jnp.einsum('bsm,bmd->bsd', attn, memory_tokens)
        valid_b = jnp.any(memory_mask, axis=-1)
        out = jnp.where(valid_b[:, None, None], readout, jnp.zeros_like(readout))
        return out

    def _L1_ffn_ref(x, w_r, b_r, w1, b1, w2, b2):
        import jax, jax.numpy as jnp
        import numpy as np
        B, L, D = (4, 512, 256)
        DF = 4 * D
        CAPACITY_RATIO = 0.5
        b, l, d = x.shape
        k = int(l * CAPACITY_RATIO)
        scores = jnp.einsum('bld,d->bl', x, w_r) + b_r
        _, idx = jax.lax.top_k(scores, k)
        x_sel = jnp.take_along_axis(x, idx[:, :, None], axis=1)
        h = jax.nn.gelu(jnp.einsum('bkd,df->bkf', x_sel, w1) + b1)
        out_sel = jnp.einsum('bkf,fd->bkd', h, w2) + b2
        batch_ix = jnp.arange(b)[:, None]
        out = jnp.zeros_like(x).at[batch_ix, idx].set(out_sel)
        return out
    x = x + _L0_xattn_ref(_layernorm(x, axis=-1), ctx_2048, ctx_2048)
    x = x + _L0_ffn_ref(_layernorm(x, axis=-1), L0_ffn_router_w, L0_ffn_router_b, L0_ffn_expert_w, L0_ffn_expert_b)
    x = x + _L1_xattn_ref(_layernorm(x, axis=-1), ctx_2048, mask_BxS2_bk0)
    x = x + _L1_ffn_ref(_layernorm(x, axis=-1), L1_ffn_w_r, L1_ffn_b_r, L1_ffn_w1, L1_ffn_b1, L1_ffn_w2, L1_ffn_b2)
    return x

_drawn_inputs = setup_inputs


def setup_inputs(seed=0):
    import zlib

    import numpy as np

    out = dict(_drawn_inputs(seed))
    spreads = {'L0_ffn_router_b': (0.0, 0.8),
     'L0_ffn_expert_b': (0.0, 0.679),
     'L1_ffn_b1': (0.0, 0.437),
     'L1_ffn_b2': (0.0, 0.1)}
    factors = {}
    for name, (base, spread) in spreads.items():
        noise = np.random.default_rng([zlib.crc32(name.encode()), seed]).standard_normal(out[name].shape)
        drawn = base * np.exp(spread * noise) if base else spread * noise
        out[name] = jnp.asarray(drawn.astype(out[name].dtype))
    for name, factor in factors.items():
        out[name] = (out[name] * factor).astype(out[name].dtype)
    return out
```

```python
from contextlib import ExitStack

import concourse.bass as bass
from concourse import mybir

F32 = mybir.dt.float32
BF16 = mybir.dt.bfloat16
I32 = mybir.dt.int32
U8 = mybir.dt.uint8
ALU = mybir.AluOpType
ACT = mybir.ActivationFunctionType
AX = mybir.AxisListType

P = 128
NB = 16
D = 256
NH = 8
C = P // NH
CA = C + 1
NU = NB // 2
STEPS = 2 * NH
NE = 16
KE = NB * P // NE
KT = P // 2
DF = 4 * D
NF = DF // P
NG = 4
EPS = 1e-5
MASKED = -1e30
SLOTS = 3
QROWS = 6 * C
SROWS = QROWS + 2
SEARCH_BITS = 30


def build_program(nc, x, ctx_2048, mask, router_w, router_b, expert_w, expert_b,
                  w_r, b_r, w1, b1, w2, b2, out):
    with ExitStack() as stack:
        def sb(name, shape, dt=F32):
            return stack.enter_context(nc.sbuf_tensor(name, shape, dt))

        def bank(name):
            return stack.enter_context(nc.psum_tensor(name, [P, 512], F32))

        def sem(name):
            return stack.enter_context(nc.semaphore(name))

        q_parts_dram = nc.dram_tensor("q_parts_dram", (NU, 3, C, NH, 2 * D), BF16, kind="Internal").ap()
        k_parts_dram = nc.dram_tensor("k_parts_dram", (NU, 3, C, NH, 2 * D), BF16, kind="Internal").ap()

        xs = sb("xs", [P, NB, D])
        ctx = sb("ctx", [P, NB, D])
        ctx_stage = sb("ctx_stage", [P, 2, D])
        x_stage = sb("x_stage", [P, 2, D])
        x_new = sb("x_new", [P, 2, D])
        x_new3 = sb("x_new3", [P, 2, D])
        vt = sb("vt", [P, NB, 2, NH, CA])
        y = sb("y", [P, NB, D])
        q_stack = sb("q_stack", [P, SLOTS, NH, 2, D], BF16)
        k_stack = sb("k_stack", [P, SLOTS, NH, 2, D], BF16)
        probs = sb("probs", [P, 4, 512])
        mv0 = sb("mv0", [P, 2, 2])
        st = sb("st", [P, 2, 6])
        var16 = sb("var16", [P, 2])
        rstd_q = sb("rstd_q", [P, 2])
        minus_half = sb("minus_half", [P, 2])
        qn = sb("qn", [P, 2, D])
        q_rest = sb("q_rest", [P, 2 * D])
        q_parts = sb("q_parts", [P, 3, 2 * D], BF16)
        k_rest = sb("k_rest", [P, 2 * D])
        k_parts = sb("k_parts", [P, 3, 2 * D], BF16)
        row_max = sb("row_max", [P, 2, 2, NH])
        neg_max = sb("neg_max", [NH, 2, 2, D], BF16)
        inv_sum = sb("inv_sum", [P, 2, 2, NH])
        yn = sb("yn", [P, 2, 2, P])
        mv = sb("mv", [P, 2, 2])
        var_eps = sb("var_eps", [P, 2])
        rstd = sb("rstd", [P, 2])
        xn = sb("xn", [P, 2, D])
        xnt = sb("xnt", [P, 2, 2, P])
        wr_moving = sb("wr_moving", [P, 2, D + NE])
        eb_rows = sb("eb_rows", [P, D + NE])
        logits = sb("logits", [P, NB, NE])
        lg_max = sb("lg_max", [P, NB])
        lg_sum = sb("lg_sum", [P, NB])
        lg_inv = sb("lg_inv", [P, NB])
        st_probs = sb("st_probs", [P, 2, P])
        ident = sb("ident", [P, P])
        ident_bf = sb("ident_bf", [P, P], BF16)
        earlier = sb("earlier", [P, P])
        same_expert = sb("same_expert", [P, P], BF16)
        earlier_batch = sb("earlier_batch", [P, P], BF16)
        batch_of = sb("batch_of", [P, NH])
        free_i = sb("free_i", [P, P], I32)
        part_i = sb("part_i", [P, 1], I32)
        work_i = sb("work_i", [P, P], I32)
        work_p = sb("work_p", [P, 2], I32)
        free_f = sb("free_f", [P, P])
        part_f = sb("part_f", [P, 1])
        free_lo = sb("free_lo", [P, P])
        free_hi = sb("free_hi", [P, P])
        part_lo = sb("part_lo", [P, 1])
        part_hi = sb("part_hi", [P, 1])
        ones = sb("ones", [P, P])
        ones_bf = sb("ones_bf", [2, 2 * D], BF16)
        junk = sb("junk", [P, 2, P])
        bits = sb("bits", [P, 2], I32)
        thr = sb("thr", [P, 1], I32)
        cand = sb("cand", [P, 1], I32)
        taken = sb("taken", [P, 1], I32)
        count = sb("count", [P, 1], BF16)
        above = sb("above", [P, 2, P])
        equal = sb("equal", [P, 2, P])
        running = sb("running", [P, 2, P])
        totals = sb("totals", [P, 2], BF16)
        base = sb("base", [P, 2])
        need = sb("need", [P, 1])
        gated = sb("gated", [P, 2, P])
        gate = sb("gate", [P, NB])
        mask_u8 = sb("mask_u8", [P, NB, P], U8)
        mask_bias = sb("mask_bias", [1, NB, P])
        valid = sb("valid", [P, NB])
        sc_max = sb("sc_max", [P, 2])
        sc_bias = sb("sc_bias", [P, 2])
        sc_sum = sb("sc_sum", [P, 2])
        sc_inv = sb("sc_inv", [P, 2])
        sc_coef = sb("sc_coef", [P, 2])
        attn = sb("attn", [P, 2, P])
        attn_t = sb("attn_t", [P, 2, P])
        st3 = sb("st3", [P, 2, 6])
        mv3 = sb("mv3", [P, 2, 2])
        var_eps3 = sb("var_eps3", [P, 2])
        rstd3 = sb("rstd3", [P, 2])
        z = sb("z", [P, 2, D])
        z_work = sb("z_work", [P, 2, D])
        wr_rows = sb("wr_rows", [P, D])
        br_rows = sb("br_rows", [P, 1])
        score0 = sb("score0", [P, 2])
        score = sb("score", [P, 2])
        rank_gt = sb("rank_gt", [P, 2])
        rank_eq = sb("rank_eq", [P, 2])
        rank = sb("rank", [P, 2])
        cmp_work = sb("cmp_work", [P, 2, P])
        pick = sb("pick", [P, 2, KT])
        pick_bf = sb("pick_bf", [P, NB, KT], BF16)
        zg = q_stack[:, 0].rearrange("p h b n -> p (h b n)").bitcast(F32).rearrange("p (k t) -> p k t", k=2)
        w1s = sb("w1s", [P, 2, DF])
        w2s = sb("w2s", [P, NF, D])
        b1s = sb("b1s", [P, NF])
        b2_rows = sb("b2_rows", [P, D])
        hid = probs[:, :, :].rearrange("p s (f t) -> p (s f) t", f=2)
        taken_out = sb("taken_out", [P, 2, D])
        pick_t = sb("pick_t", [P, 2, P])
        out_rows = y[:, 0:4, :].rearrange("p (t i) n -> p t i n", t=2)

        score_bank = [bank("score_bank0"), bank("score_bank1")]
        scoret_bank = [bank("scoret_bank0"), bank("scoret_bank1")]
        pv_bank = [bank("pv_bank0"), bank("pv_bank1")]
        t0_bank = bank("t0_bank")
        t1_bank = bank("t1_bank")

        c_bank, d_bank = score_bank, scoret_bank
        hid_bank, y_bank, put_bank = pv_bank, score_bank, scoret_bank
        pick_t_psum = t0_bank[:, 0:P // 2].bitcast(BF16)

        names = """passed kept w_ones x_loaded ctx_loaded staged parts_written stacks_loaded w_small w_big consts_dma
        iota_done ident_done consts_done ones_done q_split k_split stats_q pool_step norm_step
        scores_ready max_done scorest_ready exp_done pv_done normed yn_t max_t ctx_t vt_done neg_hi neg_done
        x1_done stats1 xn_ready xn_t xnt_copied yw_ready yw_done
        bn_q sh_exp st_t st_copied cand_ready counted totalled gt_counted gt_total eq_counted eq_total gated_ready gate_t gate_done
        c_bn c_stats c_xn c_xn_t c_xnt c_scores c_max c_bias c_exp c_attn_t c_attnt c_coef c_read c_x3
        d_bn d_stats d_z d_dot d_score d_rank d_row d_pick d_pickbf d_gath d_zg
        f_h f_gelu f_y f_taken f_pt f_ptc f_sc f_out""".split()
        s = {n: sem("s_" + n) for n in names}
        neg_loaded = [sem("s_neg_loaded0"), sem("s_neg_loaded1")]
        out_stored = [sem("s_out_stored0"), sem("s_out_stored1")]

        block = stack.enter_context(nc.Block())

        def is_first(u):
            return isinstance(u, int) and u == 0

        def wait_apart(eng, semaphore, value):
            eng.wait_ge(semaphore, value)
            eng.sem_inc(s["passed"], 1)

        @block.sync
        def _(sp):
            x_rows = x.rearrange("b c n -> c b n")
            ctx_rows = ctx_2048.rearrange("b c n -> c b n")

            def load_stage(u):
                if not is_first(u):
                    sp.wait_ge(s["ctx_t"], u)
                    sp.wait_ge(s["k_split"], u)
                    sp.wait_ge(s["q_split"], u)
                sp.dma_start(ctx_stage[:, :, :], ctx_rows[:, bass.ds(2 * u, 2), :]).then_inc(s["staged"], 16)
                sp.dma_start(x_stage[:, :, :], x_rows[:, bass.ds(2 * u, 2), :]).then_inc(s["staged"], 16)

            def write_parts(u):
                sp.wait_ge(s["k_split"], u + 1)
                for part in range(3):
                    sp.dma_start(k_parts_dram[u, part].rearrange("d h n -> h d n"),
                                 k_parts[:, part, :]).then_inc(s["parts_written"], 16)
                sp.wait_ge(s["q_split"], u + 1)
                for part in range(3):
                    sp.dma_start(q_parts_dram[u, part].rearrange("d h n -> h d n"),
                                 q_parts[:, part, :]).then_inc(s["parts_written"], 16)

            def load_stacks(u, reused):
                slot = u % SLOTS
                wait_apart(sp, s["parts_written"], 96 * (u + 1))
                if not is_first(u):
                    wait_apart(sp, s["stacks_loaded"], 96 * u)
                if reused:
                    wait_apart(sp, s["scorest_ready"], STEPS * (u - SLOTS + 1))
                k_rows = k_parts_dram[u].rearrange("p d h n -> (p d) (h n)")
                q_rows = q_parts_dram[u].rearrange("p d h n -> p d (h n)")
                k_to = k_stack[:, slot].rearrange("p h b n -> p (h b n)")
                q_to = q_stack[:, slot].rearrange("p h b n -> p (h b n)")
                n = NH * 2 * D
                sp.dma_start(k_to[0:3 * C], k_rows).then_inc(s["stacks_loaded"], 16)
                sp.dma_start(k_to[3 * C:5 * C], k_rows[0:2 * C]).then_inc(s["stacks_loaded"], 16)
                sp.dma_start(k_to[5 * C:6 * C], k_rows[0:C]).then_inc(s["stacks_loaded"], 16)
                sp.dma_start(q_to[0:3 * C], q_rows[0:1].to_broadcast([3, C, n])).then_inc(s["stacks_loaded"], 16)
                sp.dma_start(q_to[3 * C:5 * C], q_rows[1:2].to_broadcast([2, C, n])).then_inc(s["stacks_loaded"], 16)
                sp.dma_start(q_to[5 * C:6 * C], q_rows[2]).then_inc(s["stacks_loaded"], 16)

            def load_neg_max(u, i):
                wait_apart(sp, s["neg_done"], 2 * u + i + 1)
                for part in range(2):
                    sp.dma_start(q_stack[QROWS + part:QROWS + part + 1, u % SLOTS, :, i, :],
                                 neg_max[:, i, part, :]).then_inc(neg_loaded[i], 16)

            load_stage(0)
            sp.wait_ge(s["ones_done"], 1)
            sp.dma_start(k_stack[QROWS:SROWS].rearrange("p s h b n -> p (s h) (b n)"),
                         ones_bf[:, :].unsqueeze(1).to_broadcast([2, SLOTS * NH, 2 * D])).then_inc(s["w_ones"], 16)
            sp.dma_start(xs[:, :, :], x_rows).then_inc(s["x_loaded"], 16)
            sp.dma_start(ctx[:, :, :], ctx_rows).then_inc(s["ctx_loaded"], 16)
            for half in range(2):
                sp.dma_start(wr_moving[:, half, 0:D], expert_w[half * P:(half + 1) * P, :]).then_inc(s["w_small"], 16)
                sp.dma_start(wr_moving[:, half, D:D + NE], router_w[half * P:(half + 1) * P, :]).then_inc(s["w_small"], 16)
            for dst, row in ((eb_rows[:, 0:D], expert_b), (eb_rows[:, D:D + NE], router_b),
                             (wr_rows[:, :], w_r), (b2_rows[:, :], b2)):
                sp.dma_start(dst, row.rearrange("(a n) -> a n", a=1).to_broadcast([P, row.shape[0]])).then_inc(s["w_small"], 16)
            sp.dma_start(br_rows[:, :], b_r.to_broadcast([P, 1])).then_inc(s["w_small"], 16)
            sp.dma_start(mask_u8[:, :, :], mask.rearrange("(a b) m -> a b m", a=1).to_broadcast([P, NB, P])).then_inc(s["w_small"], 16)
            write_parts(0)
            load_stage(1)
            load_stacks(0, False)
            write_parts(1)
            load_stage(2)
            load_stacks(1, False)
            load_neg_max(0, 0)
            sp.dma_start(w1s[:, :, :], w1.rearrange("(k p) f -> p k f", p=P)).then_inc(s["w_big"], 16)
            sp.dma_start(w2s[:, :, :], w2.rearrange("(k p) f -> p k f", p=P)).then_inc(s["w_big"], 16)
            with nc.allow_non_contiguous_dma(reason="1024 single biases, one per partition and block"):
                sp.dma_start(b1s[:, :], b1.rearrange("(k p) -> p k", p=P)).then_inc(s["w_big"], 16)

            def unit(u, more_stage, more_parts, more_max, reused):
                load_neg_max(u, 1)
                if more_parts:
                    write_parts(u + 2)
                    if more_stage:
                        load_stage(u + 3)
                    load_stacks(u + 2, reused)
                if more_max:
                    load_neg_max(u + 1, 0)

            unit(0, True, True, True, False)
            unit(1, True, True, True, True)
            with sp.Fori(2, NU - 3) as u:
                unit(u, True, True, True, True)
            unit(NU - 3, False, True, True, True)
            unit(NU - 2, False, False, True, True)
            unit(NU - 1, False, False, False, True)

            with sp.Fori(0, NG) as g:
                for pair in range(2):
                    sp.wait_ge(s["f_out"], 4 * g + 2 * pair + 2)
                    sp.dma_start(out.rearrange("b t n -> t b n")[:, bass.ds(4 * g + 2 * pair, 2), :],
                                 out_rows[:, pair]).then_inc(out_stored[pair], 16)
            for pair in range(2):
                sp.wait_ge(out_stored[pair], 16 * NG)

        @block.gpsimd
        def _(pool):
            pool.iota(free_i[:, :], pattern=[[1, P]], base=0, channel_multiplier=0).then_inc(s["iota_done"], 1)
            pool.wait_ge(s["iota_done"], 1)
            pool.iota(part_i[:, :], pattern=[[0, 1]], base=0, channel_multiplier=1).then_inc(s["iota_done"], 1)
            pool.wait_ge(s["ones_done"], 1)

            steps = 9

            def split_unit(u):
                n = [0]

                def link(ins):
                    n[0] += 1
                    ins.then_inc(s["pool_step"], 1)
                    wait_apart(pool, s["pool_step"], steps * u + n[0])

                if not is_first(u):
                    pool.wait_ge(s["parts_written"], 96 * u)
                wait_apart(pool, s["staged"], 32 * (u + 1))
                pair = ctx_stage[:, :, :].rearrange("p b n -> p (b n)")
                link(pool.tensor_copy(k_parts[:, 0, :], pair))
                link(pool.tensor_tensor(k_rest[:, :], pair, k_parts[:, 0, :], ALU.subtract))
                link(pool.tensor_copy(k_parts[:, 1, :], k_rest[:, :]))
                pool.tensor_tensor(k_parts[:, 2, :], k_rest[:, :], k_parts[:, 1, :], ALU.subtract).then_inc(s["k_split"], 1)
                wait_apart(pool, s["stats_q"], u + 1)
                link(pool.tensor_scalar(var16[:, :], mv0[:, :, 1], EPS, float(C), ALU.add, ALU.mult))
                link(pool.tensor_tensor(rstd_q[:, :], var16[:, :], minus_half[:, :], ALU.pow))
                for i in range(2):
                    ins = pool.tensor_scalar(qn[:, i, :], x_stage[:, i, :], mv0[:, i, 0:1], rstd_q[:, i:i + 1],
                                             ALU.subtract, ALU.mult)
                link(ins)
                flat = qn[:, :, :].rearrange("p b n -> p (b n)")
                link(pool.tensor_copy(q_parts[:, 0, :], flat))
                link(pool.tensor_tensor(q_rest[:, :], flat, q_parts[:, 0, :], ALU.subtract))
                link(pool.tensor_copy(q_parts[:, 1, :], q_rest[:, :]))
                pool.tensor_tensor(q_parts[:, 2, :], q_rest[:, :], q_parts[:, 1, :], ALU.subtract).then_inc(s["q_split"], 1)
                assert n[0] == steps

            def keep_rows(rows, b, i):
                pool.tensor_copy(xs[:, b, :], rows[:, i, :]).then_inc(s["kept"], 1)

            def normalise(b, i, first):
                wait_apart(pool, s["stats1"], b + 1)
                pool.tensor_scalar(var_eps[:, i:i + 1], mv[:, i, 1:2], EPS, None, ALU.add).then_inc(s["norm_step"], 1)
                wait_apart(pool, s["norm_step"], 2 * b + 1)
                pool.tensor_tensor(rstd[:, i:i + 1], var_eps[:, i:i + 1], minus_half[:, 0:1], ALU.pow).then_inc(s["norm_step"], 1)
                if not first:
                    pool.wait_ge(s["xn_t"], b - 1)
                wait_apart(pool, s["norm_step"], 2 * b + 2)
                pool.tensor_scalar(xn[:, i, :], x_new[:, i, :], mv[:, i, 0:1], rstd[:, i:i + 1],
                                   ALU.subtract, ALU.mult).then_inc(s["xn_ready"], 1)
                keep_rows(x_new, b, i)

            split_unit(0)
            split_unit(1)
            split_unit(2)
            split_unit(3)
            for i in range(2):
                normalise(i, i, True)
            with pool.Fori(2, NU - 2) as u:
                split_unit(u + 2)
                for i in range(2):
                    normalise(2 * (u - 1) + i, i, False)
            for u in (NU - 2, NU - 1, NU):
                for i in range(2):
                    normalise(2 * (u - 1) + i, i, False)

            def rows3(b, i, stats, done, free, var, r, m, rows, dst, first):
                wait_apart(pool, s[stats], b + 1)
                base = 3 * b
                pool.tensor_scalar(var[:, i:i + 1], m[:, i, 1:2], EPS, None, ALU.add).then_inc(s[done], 1)
                wait_apart(pool, s[done], base + 1)
                pool.tensor_tensor(r[:, i:i + 1], var[:, i:i + 1], minus_half[:, 0:1], ALU.pow).then_inc(s[done], 1)
                if not first:
                    pool.wait_ge(s[free], b - 1)
                wait_apart(pool, s[done], base + 2)
                pool.tensor_scalar(dst[:, i, :], rows[:, i, :], m[:, i, 0:1], r[:, i:i + 1],
                                   ALU.subtract, ALU.mult).then_inc(s[done], 1)

            def pair_c(v, first):
                for i in range(2):
                    rows3(2 * v + i, i, "c_stats", "c_xn", "c_xn_t", var_eps, rstd, mv, x_new, xn, first)

            def pair_d(v, first):
                for i in range(2):
                    rows3(2 * v + i, i, "d_stats", "d_z", "d_gath", var_eps3, rstd3, mv3, x_new3, z, first)
                    keep_rows(x_new3, 2 * v + i, i)
                for i in range(2):
                    b = 2 * v + i
                    wait_apart(pool, s["d_pick"], b + 1)
                    pool.tensor_copy(pick_bf[:, b, :], pick[:, i, :]).then_inc(s["d_pickbf"], 1)

            pair_c(0, True)
            pair_c(1, False)
            pair_d(0, True)
            with pool.Fori(2, NU) as v:
                pair_c(v, False)
                pair_d(v - 1, False)
            pair_d(NU - 1, False)

        @block.vector
        def _(dve):
            dve.memset(minus_half[:, :], -0.5)
            dve.memset(vt[:, :, :, :, C:CA], 1.0)
            dve.memset(ones[:, :], 1.0)
            dve.memset(ones_bf[:, :], 1.0).then_inc(s["ones_done"], 1)
            dve.wait_ge(s["iota_done"], 2)
            k = [0]

            def link(ins):
                k[0] += 1
                ins.then_inc(s["consts_done"], 1)
                dve.wait_ge(s["consts_done"], k[0])

            dve.tensor_copy(free_f[:, :], free_i[:, :])
            link(dve.tensor_copy(part_f[:, :], part_i[:, :]))
            dve.tensor_scalar(ident[:, :], free_f[:, :], part_f[:, 0:1], None, ALU.is_equal).then_inc(s["ident_done"], 1)
            dve.wait_ge(s["ident_done"], 1)

            def stats_q(u):
                if not is_first(u):
                    dve.wait_ge(s["q_split"], u)
                dve.wait_ge(s["staged"], 32 * (u + 1))
                for i in range(2):
                    dve.bn_stats(st[:, i, :], x_stage[:, i, :]).then_inc(s["bn_q"], 1)
                wait_apart(dve, s["bn_q"], 2 * u + 2)
                dve.bn_aggr(mv0[:, 0, :], st[:, 0, :])
                dve.bn_aggr(mv0[:, 1, :], st[:, 1, :]).then_inc(s["stats_q"], 1)

            stats_q(0)
            link(dve.tensor_scalar(earlier[:, :], free_f[:, :], part_f[:, 0:1], None, ALU.is_lt))
            dve.tensor_copy(ident_bf[:, :], ident[:, :])
            link(dve.tensor_scalar(work_i[:, :], free_i[:, :], 15, None, ALU.bitwise_and))
            link(dve.tensor_scalar(work_p[:, 0:1], part_i[:, :], 15, None, ALU.bitwise_and))
            link(dve.tensor_scalar(work_p[:, 1:2], part_i[:, :], 4, None, ALU.logical_shift_right))
            dve.tensor_copy(free_lo[:, :], work_i[:, :])
            dve.tensor_copy(part_lo[:, :], work_p[:, 0:1])
            link(dve.tensor_copy(part_hi[:, :], work_p[:, 1:2]))
            link(dve.tensor_scalar(work_i[:, :], free_i[:, :], 4, None, ALU.logical_shift_right))
            link(dve.tensor_copy(free_hi[:, :], work_i[:, :]))
            dve.tensor_scalar(batch_of[:, :], free_f[:, 0:NH], part_hi[:, 0:1], None, ALU.is_equal)
            link(dve.tensor_scalar(same_expert[:, :], free_lo[:, :], part_lo[:, 0:1], None, ALU.is_equal))
            link(dve.scalar_tensor_tensor(earlier_batch[:, :], free_hi[:, :], part_hi[:, 0:1], same_expert[:, :],
                                          ALU.is_gt, ALU.mult))
            n_consts = k[0]
            stats_q(1)

            def maximum(step, b, h, i, first_h):
                if first_h:
                    dve.wait_ge(s["max_t"], b - 1)
                dve.wait_ge(s["scores_ready"], step + 1)
                dve.tensor_reduce(row_max[:, i, :, h], score_bank[h % 2][:, :].rearrange("p (m n) -> p m n", m=2),
                                  AX.X, ALU.max).then_inc(s["max_done"], 1)

            def neg_low(b, i):
                dve.wait_ge(s["neg_hi"], b + 1)
                dve.scalar_tensor_tensor(neg_max[:, i, 1, :], t0_bank[0:NH, 0:D], -1.0, neg_max[:, i, 0, :],
                                         ALU.mult, ALU.subtract).then_inc(s["neg_done"], 1)

            def norm(b, i, first):
                o = pv_bank[i][:, 0:2 * NH * CA].rearrange("p (m h c) -> p m h c", m=2, h=NH)
                dve.wait_ge(s["pv_done"], NH * (b + 1))
                dve.reciprocal(inv_sum[:, i], o[:, :, :, C]).then_inc(s["normed"], 1)
                dve.wait_ge(s["normed"], 2 * b + 1)
                if not first:
                    dve.wait_ge(s["yn_t"], b - 1)
                dve.tensor_tensor(yn[:, i].rearrange("p m (h c) -> p m h c", h=NH), o[:, :, :, 0:C],
                                  inv_sum[:, i].unsqueeze(3).to_broadcast([P, 2, NH, C]), ALU.mult).then_inc(s["normed"], 1)

            def add_x1(b, i, first=False):
                dve.wait_ge(s["yn_t"], b + 1)
                if not first:
                    dve.wait_ge(s["kept"], b - 1)
                dve.tensor_tensor(x_new[:, i, :], t1_bank[:, 0:D], xs[:, b, :], ALU.add).then_inc(s["x1_done"], 1)
                dve.wait_ge(s["x1_done"], 2 * b + 1)
                dve.bn_stats(st3[:, i, :], x_new[:, i, :]).then_inc(s["x1_done"], 1)
                wait_apart(dve, s["x1_done"], 2 * b + 2)
                dve.bn_aggr(mv[:, i, :], st3[:, i, :]).then_inc(s["stats1"], 1)

            def take_yw(b):
                dve.wait_ge(s["yw_ready"], b + 1)
                dve.tensor_tensor(y[:, b, :], t1_bank[:, 0:D], eb_rows[:, 0:D], ALU.add)
                dve.tensor_tensor(logits[:, b, :], t1_bank[:, D:D + NE], eb_rows[:, D:D + NE], ALU.add).then_inc(s["yw_done"], 1)

            def unit(u, first, last, stats):
                for j in range(STEPS):
                    if j == 0 and not first:
                        norm(2 * u - 1, 1, isinstance(u, int) and u == 1)
                    if j == 1 and stats:
                        stats_q(u + 2)
                    if not last:
                        maximum(STEPS * (u + 1) + j, 2 * (u + 1) + j // NH, j % NH, j // NH, j % NH == 0)
                    if j == 2:
                        neg_low(2 * u + 1, 1)
                    if j == 3 and not first:
                        add_x1(2 * u - 2, 0, isinstance(u, int) and u == 1)
                    if j == 5 and not first:
                        add_x1(2 * u - 1, 1, isinstance(u, int) and u == 1)
                    if j == 9:
                        norm(2 * u, 0, first)
                    if j == 11 and not last:
                        neg_low(2 * u + 2, 0)
                    if j == 14 and not first:
                        take_yw(2 * u - 2)
                    if j == 15 and not first:
                        take_yw(2 * u - 1)

            for j in range(2):
                maximum(j, 0, j, 0, False)
            with dve.Fori(1, NH // 2) as q:
                for j in range(2):
                    dve.wait_ge(s["scores_ready"], 2 * q + j + 1)
                    dve.tensor_reduce(row_max[:, 0, :, 2 * q + j],
                                      score_bank[j][:, :].rearrange("p (m n) -> p m n", m=2),
                                      AX.X, ALU.max).then_inc(s["max_done"], 1)
            neg_low(0, 0)
            with dve.Fori(0, NH // 2) as q:
                for j in range(2):
                    dve.wait_ge(s["scores_ready"], NH + 2 * q + j + 1)
                    dve.tensor_reduce(row_max[:, 1, :, 2 * q + j],
                                      score_bank[j][:, :].rearrange("p (m n) -> p m n", m=2),
                                      AX.X, ALU.max).then_inc(s["max_done"], 1)
            dve.wait_ge(s["w_small"], 16 * 10)
            dve.tensor_scalar(mask_bias[:, :, :], mask_u8[0:1, :, :], -1.0, -MASKED, ALU.add, ALU.mult)
            dve.tensor_reduce(valid[:, :], mask_u8[:, :, :], AX.X, ALU.max)
            dve.wait_ge(s["x_loaded"], 16)
            unit(0, True, False, True)
            unit(1, False, False, True)
            with dve.Fori(2, NU - 2) as u:
                unit(u, False, False, True)
            unit(NU - 2, False, False, False)
            unit(NU - 1, False, True, False)
            norm(NB - 1, 1, False)
            add_x1(NB - 2, 0)
            add_x1(NB - 1, 1)
            take_yw(NB - 2)
            take_yw(NB - 1)

            k[0] = n_consts
            dve.wait_ge(s["yw_done"], NB)
            link(dve.tensor_reduce(lg_max[:, :], logits[:, :, :], AX.X, ALU.max))
            dve.tensor_tensor(logits[:, :, :], logits[:, :, :], lg_max[:, :].unsqueeze(2).to_broadcast([P, NB, NE]),
                              ALU.subtract).then_inc(s["sh_exp"], 1)
            dve.wait_ge(s["sh_exp"], 2)
            link(dve.tensor_reduce(lg_sum[:, :], logits[:, :, :], AX.X, ALU.add))
            link(dve.reciprocal(lg_inv[:, :], lg_sum[:, :]))
            dve.tensor_tensor(logits[:, :, :], logits[:, :, :], lg_inv[:, :].unsqueeze(2).to_broadcast([P, NB, NE]),
                              ALU.mult).then_inc(s["sh_exp"], 1)
            link(dve.memset(thr[:, :], 0))
            dve.memset(cand[:, :], 1 << (SEARCH_BITS - 1))
            dve.memset(bits[:, 0:1], 1 << (SEARCH_BITS - 1))
            link(dve.memset(bits[:, 1:2], 1 << (SEARCH_BITS - 2)))
            dve.wait_ge(s["st_t"], 1)
            link(dve.tensor_copy(st_probs[:, :, :], t0_bank[:, 0:2 * P].rearrange("p (g t) -> p g t", g=2)))
            with dve.Fori(0, SEARCH_BITS) as n:
                dve.tensor_scalar(junk[:, :, :], st_probs[:, :, :], cand[:, :].bitcast(F32), None, ALU.is_ge, ALU.add,
                                  accum_out=count[:, :]).then_inc(s["counted"], 1)
                dve.wait_ge(s["totalled"], n + 1)
                dve.scalar_tensor_tensor(taken[:, :], t1_bank[:, 0:1], float(KE), bits[:, 0:1],
                                         ALU.is_ge, ALU.mult).then_inc(s["cand_ready"], 1)
                dve.wait_ge(s["cand_ready"], 3 * n + 1)
                dve.scalar_tensor_tensor(cand[:, :], taken[:, :], thr[:, 0:1], bits[:, 1:2],
                                         ALU.bitwise_or, ALU.bitwise_or).then_inc(s["cand_ready"], 1)
                dve.wait_ge(s["cand_ready"], 3 * n + 2)
                dve.tensor_tensor(thr[:, :], thr[:, :], taken[:, :], ALU.bitwise_or)
                dve.tensor_scalar(bits[:, :], bits[:, :], 1, None, ALU.logical_shift_right).then_inc(s["cand_ready"], 1)
                dve.wait_ge(s["cand_ready"], 3 * n + 3)
            threshold = thr[:, :].bitcast(F32)
            dve.tensor_scalar(above[:, :, :], st_probs[:, :, :], threshold, None, ALU.is_gt, ALU.add,
                              accum_out=count[:, :]).then_inc(s["counted"], 1)
            link(dve.tensor_scalar(equal[:, :, :], st_probs[:, :, :], threshold, None, ALU.is_equal))
            for g in range(2):
                link(dve.tensor_tensor_scan(running[:, g, :], ones[:, :], equal[:, g, :], 0.0, ALU.mult, ALU.add))
            dve.tensor_copy(totals[:, :], running[:, :, P - 1]).then_inc(s["eq_counted"], 1)
            dve.wait_ge(s["gt_total"], 1)
            dve.wait_ge(s["eq_total"], 1)
            link(dve.tensor_scalar(need[:, :], t1_bank[:, 1:2], -1.0, float(KE), ALU.mult, ALU.add))
            link(dve.tensor_copy(base[:, :], t1_bank[:, 2:4]))
            link(dve.tensor_tensor(base[:, 1:2], t1_bank[:, 4:5], base[:, 1:2], ALU.add))
            for g in range(2):
                link(dve.tensor_scalar(running[:, g, :], running[:, g, :], base[:, g:g + 1], need[:, 0:1], ALU.add, ALU.is_le))
            link(dve.tensor_tensor(equal[:, :, :], equal[:, :, :], running[:, :, :], ALU.mult))
            link(dve.tensor_tensor(above[:, :, :], above[:, :, :], equal[:, :, :], ALU.add))
            dve.tensor_tensor(gated[:, :, :], above[:, :, :], st_probs[:, :, :], ALU.mult).then_inc(s["gated_ready"], 1)
            dve.wait_ge(s["gate_t"], 1)
            link(dve.tensor_copy(gate[:, :], t0_bank[:, 0:NB]))

            def c_stats(b, i, first):
                if first:
                    dve.wait_ge(s["kept"], NB)
                else:
                    dve.wait_ge(s["c_x3"], b - 1)
                dve.scalar_tensor_tensor(x_new[:, i, :], y[:, b, :], gate[:, bass.ds(b, 1)], xs[:, b, :],
                                         ALU.mult, ALU.add).then_inc(s["c_bn"], 1)
                dve.wait_ge(s["c_bn"], 2 * b + 1)
                dve.bn_stats(st[:, i, :], x_new[:, i, :]).then_inc(s["c_bn"], 1)
                wait_apart(dve, s["c_bn"], 2 * b + 2)
                dve.bn_aggr(mv[:, i, :], st[:, i, :]).then_inc(s["c_stats"], 1)

            def c_max(b, i):
                dve.wait_ge(s["c_scores"], b + 1)
                dve.tensor_reduce(sc_max[:, i:i + 1], c_bank[i][:, 256:384], AX.X, ALU.max).then_inc(s["c_max"], 1)
                dve.wait_ge(s["c_max"], b + 1)
                dve.tensor_scalar(sc_bias[:, i:i + 1], sc_max[:, i:i + 1], -(D ** -0.5), None,
                                  ALU.mult).then_inc(s["c_bias"], 1)

            def c_add(b, i, first):
                dve.wait_ge(s["c_exp"], b + 1)
                dve.reciprocal(sc_inv[:, i:i + 1], sc_sum[:, i:i + 1]).then_inc(s["c_coef"], 1)
                dve.wait_ge(s["c_coef"], 2 * b + 1)
                dve.tensor_tensor(sc_coef[:, i:i + 1], sc_inv[:, i:i + 1], valid[:, bass.ds(b, 1)],
                                  ALU.mult).then_inc(s["c_coef"], 1)
                dve.wait_ge(s["c_coef"], 2 * b + 2)
                dve.wait_ge(s["c_read"], b + 1)
                if not first:
                    dve.wait_ge(s["kept"], NB + b - 1)
                dve.scalar_tensor_tensor(x_new3[:, i, :], c_bank[i][:, 0:D], sc_coef[:, i:i + 1], x_new[:, i, :],
                                         ALU.mult, ALU.add).then_inc(s["c_x3"], 1)

            def d_stats(b, i):
                dve.wait_ge(s["c_x3"], b + 1)
                dve.bn_stats(st3[:, i, :], x_new3[:, i, :]).then_inc(s["d_bn"], 1)
                wait_apart(dve, s["d_bn"], b + 1)
                dve.bn_aggr(mv3[:, i, :], st3[:, i, :]).then_inc(s["d_stats"], 1)

            def d_score(b, i):
                dve.wait_ge(s["d_z"], 3 * b + 3)
                dve.tensor_tensor_reduce(out=z_work[:, i, :], in0=z[:, i, :], in1=wr_rows[:, :], scale=1.0, scalar=0.0,
                                         op0=ALU.mult, op1=ALU.add, accum_out=score0[:, i:i + 1]).then_inc(s["d_dot"], 1)
                dve.wait_ge(s["d_dot"], b + 1)
                dve.tensor_tensor(score[:, i:i + 1], score0[:, i:i + 1], br_rows[:, :], ALU.add).then_inc(s["d_score"], 1)

            def d_pick(b, i, first):
                row = d_bank[i][:, 0:P]
                dve.wait_ge(s["d_row"], b + 1)
                dve.tensor_scalar(cmp_work[:, i, :], row, score[:, i:i + 1], None, ALU.is_gt, ALU.add,
                                  accum_out=rank_gt[:, i:i + 1]).then_inc(s["d_rank"], 1)
                dve.wait_ge(s["d_rank"], 3 * b + 1)
                dve.scalar_tensor_tensor(cmp_work[:, i, :], row, score[:, i:i + 1], earlier[:, :], ALU.is_equal, ALU.mult,
                                         accum_out=rank_eq[:, i:i + 1]).then_inc(s["d_rank"], 1)
                dve.wait_ge(s["d_rank"], 3 * b + 2)
                dve.tensor_tensor(rank[:, i:i + 1], rank_gt[:, i:i + 1], rank_eq[:, i:i + 1], ALU.add).then_inc(s["d_rank"], 1)
                dve.wait_ge(s["d_rank"], 3 * b + 3)
                if not first:
                    dve.wait_ge(s["d_gath"], b - 1)
                    dve.wait_ge(s["d_pickbf"], b - 1)
                dve.tensor_scalar(pick[:, i, :], free_f[:, 0:KT], rank[:, i:i + 1], None, ALU.is_equal).then_inc(s["d_pick"], 1)

            def pair(v, c, d, first_d):
                if c:
                    for i in range(2):
                        c_stats(2 * v + i, i, is_first(v))
                if d:
                    for i in range(2):
                        d_stats(2 * v - 2 + i, i)
                if c:
                    for i in range(2):
                        c_max(2 * v + i, i)
                if d:
                    for i in range(2):
                        d_score(2 * v - 2 + i, i)
                if c:
                    for i in range(2):
                        c_add(2 * v + i, i, is_first(v))
                if d:
                    for i in range(2):
                        d_pick(2 * v - 2 + i, i, first_d)

            pair(0, True, False, False)
            pair(1, True, True, True)
            with dve.Fori(2, NU) as v:
                pair(v, True, True, False)
            pair(NU, False, True, False)

            dve.wait_ge(s["kept"], 2 * NB)

            def group(g, first):
                for t in range(2):
                    if not first:
                        dve.wait_ge(s["f_sc"], 4 * g)
                    dve.wait_ge(s["f_y"], 2 * g + t + 1)
                    dve.tensor_tensor(taken_out[:, t, :], y_bank[t][:, 0:D], b2_rows[:, :], ALU.add).then_inc(s["f_taken"], 1)
                for t in range(2):
                    if not first:
                        dve.wait_ge(out_stored[t], 16 * g)
                    for i in range(2):
                        dve.wait_ge(s["f_sc"], 4 * g + 2 * t + i + 1)
                        dve.tensor_tensor(out_rows[:, t, i, :], put_bank[i][:, 0:D], xs[:, 4 * g + 2 * t + i, :],
                                          ALU.add).then_inc(s["f_out"], 1)

            group(0, True)
            with dve.Fori(1, NG) as g:
                group(g, False)

        @block.scalar
        def _(act):
            def exponential(t, j, first):
                act.wait_ge(s["scorest_ready"], t + 1)
                if not first:
                    act.wait_ge(s["pv_done"], t - 3)
                act.activation(probs[:, j % 4, :], scoret_bank[j % 2][:, :], ACT.Exp).then_inc(s["exp_done"], 1)

            def neg_high(b, u, i):
                act.wait_ge(s["max_t"], b + 1)
                if not is_first(u):
                    act.wait_ge(neg_loaded[i], 32 * u)
                act.mul(neg_max[:, i, 0, :], t0_bank[0:NH, 0:D], -1.0).then_inc(s["neg_hi"], 1)

            def take_vt(u):
                act.wait_ge(s["ctx_t"], u + 1)
                act.copy(vt[:, bass.ds(2 * u, 2), :, :, 0:C].rearrange("p b k h c -> p (b k) h c"),
                         t0_bank[:, :].rearrange("p (k h c) -> p k h c", k=4, h=NH)).then_inc(s["vt_done"], 1)

            def take_xnt(b, i, first):
                act.wait_ge(s["xn_t"], b + 1)
                if not first:
                    act.wait_ge(s["yw_ready"], b - 1)
                act.copy(xnt[:, i].rearrange("p k t -> p (k t)"), t1_bank[:, 0:D]).then_inc(s["xnt_copied"], 1)

            act.wait_ge(s["ones_done"], 1)
            take_vt(0)
            take_vt(1)
            neg_high(0, 0, 0)

            def unit(u, first, second, last, vt_left=True):
                for j in range(STEPS):
                    exponential(STEPS * u + j, j, first and j < 4)
                    if j == 0:
                        neg_high(2 * u + 1, u, 1)
                    if j == 6 and vt_left:
                        take_vt(u + 2)
                    if j == 10 and not last:
                        neg_high(2 * u + 2, u + 1, 0)
                    if j == 11 and not first:
                        take_xnt(2 * u - 2, 0, second)
                    if j == 13 and not first:
                        take_xnt(2 * u - 1, 1, second)

            unit(0, True, False, False)
            unit(1, False, True, False)
            with act.Fori(2, NU - 2) as u:
                unit(u, False, False, False)
            unit(NU - 2, False, False, False, False)
            unit(NU - 1, False, False, True, False)
            take_xnt(NB - 2, 0, False)
            take_xnt(NB - 1, 1, False)

            act.wait_ge(s["sh_exp"], 1)
            act.activation(logits[:, :, :], logits[:, :, :], ACT.Exp).then_inc(s["sh_exp"], 1)

            def pair(v, c, d, first):
                if c:
                    for i in range(2):
                        act.wait_ge(s["c_xn_t"], 2 * v + i + 1)
                        if not first:
                            act.wait_ge(s["c_scores"], 2 * v + i - 1)
                        act.copy(xnt[:, i].rearrange("p k t -> p (k t)"), c_bank[i][:, 0:D]).then_inc(s["c_xnt"], 1)
                    for i in range(2):
                        act.wait_ge(s["c_bias"], 2 * v + i + 1)
                        if not first:
                            act.wait_ge(s["c_attn_t"], 2 * v + i - 1)
                            act.wait_ge(s["c_coef"], 4 * v + 2 * i - 2)
                        act.activation(attn[:, i, :], c_bank[i][:, 256:384], ACT.Exp, bias=sc_bias[:, i:i + 1],
                                       scale=D ** -0.5, accum_out=sc_sum[:, i:i + 1]).then_inc(s["c_exp"], 1)
                    for i in range(2):
                        act.wait_ge(s["c_attn_t"], 2 * v + i + 1)
                        if not first:
                            act.wait_ge(s["c_read"], 2 * v + i - 1)
                        act.copy(attn_t[:, i, :], c_bank[i][:, 384:512]).then_inc(s["c_attnt"], 1)
                if d:
                    for i in range(2):
                        b = 2 * v - 2 + i
                        act.wait_ge(s["d_gath"], b + 1)
                        act.copy(zg[:, :, bass.ds(KT * b, KT)],
                                 d_bank[i][:, P:2 * P].rearrange("p (k t) -> p k t", k=2)).then_inc(s["d_zg"], 1)

            pair(0, True, False, True)
            with act.Fori(1, NU) as v:
                pair(v, True, True, False)
            pair(NU, False, True, False)

            def group(g, first):
                for t in range(2):
                    act.wait_ge(s["f_pt"], 2 * g + t + 1)
                    if not first:
                        act.wait_ge(s["f_sc"], 4 * g)
                    act.copy(pick_t[:, t, :], pick_t_psum).then_inc(s["f_ptc"], 1)
                if not first:
                    act.wait_ge(s["f_y"], 2 * g)
                for f in range(NF):
                    act.wait_ge(s["f_h"], NF * g + f + 1)
                    act.activation(hid[:, f, :], hid_bank[f % 2][:, 0:4 * KT], ACT.Gelu_apprx_tanh,
                                   bias=b1s[:, f:f + 1]).then_inc(s["f_gelu"], 1)

            group(0, True)
            with act.Fori(1, NG) as g:
                group(g, False)

        @block.tensor
        def _(pe):
            def scores(step, u, b_in, h, free):
                if free is not None:
                    pe.wait_ge(s["max_done"], free)
                slot = u % SLOTS
                for m in range(2):
                    ins = pe.matmul(score_bank[h % 2][:, m * D:(m + 1) * D],
                                    q_stack[0:QROWS, slot, h, b_in, m * P:(m + 1) * P],
                                    k_stack[0:QROWS, slot, h, b_in, :], start=True, stop=True)
                ins.then_inc(s["scores_ready"], 1)

            def scores_t(t, u, j, free):
                b_in, h = j // NH, j % NH
                if free:
                    pe.wait_ge(s["exp_done"], t - 1)
                if h == 0:
                    pe.wait_ge(neg_loaded[b_in], 32 * (u + 1))
                slot = u % SLOTS
                for k in range(2):
                    ins = pe.matmul(scoret_bank[j % 2][:, k * D:(k + 1) * D],
                                    k_stack[0:SROWS, slot, h, b_in, k * P:(k + 1) * P],
                                    q_stack[0:SROWS, slot, h, b_in, :], start=True, stop=True)
                ins.then_inc(s["scorest_ready"], 1)

            def values(t, b, j, first):
                i, h = j // NH, j % NH
                if h == 0 and not first:
                    pe.wait_ge(s["normed"], 2 * (b - 1))
                pe.wait_ge(s["exp_done"], t + 1)
                o = pv_bank[i][:, 0:2 * NH * CA].rearrange("p (m h c) -> p m h c", m=2, h=NH)
                for m in range(2):
                    for k in range(2):
                        ins = pe.matmul(o[:, m, h, :], probs[:, j % 4, k * D + m * P:k * D + (m + 1) * P],
                                        vt[:, b, k, h, :], start=(k == 0), stop=(k == 1))
                ins.then_inc(s["pv_done"], 1)

            def max_t(b, i):
                pe.wait_ge(s["max_done"], NH * (b + 1))
                for m in range(2):
                    ins = pe.transpose(t0_bank[0:NH, m * P:(m + 1) * P], row_max[:, i, m, :], ident[:, :])
                ins.then_inc(s["max_t"], 1)

            def ctx_t(u):
                pe.wait_ge(s["staged"], 32 * (u + 1))
                for i in range(2):
                    for k in range(2):
                        ins = pe.transpose(t0_bank[:, (2 * i + k) * P:(2 * i + k + 1) * P],
                                           ctx_stage[:, i, k * P:(k + 1) * P], ident[:, :])
                ins.then_inc(s["ctx_t"], 1)

            def yn_t(b, i):
                pe.wait_ge(s["normed"], 2 * b + 2)
                for m in range(2):
                    ins = pe.transpose(t1_bank[:, m * P:(m + 1) * P], yn[:, i, m, :], ident[:, :])
                ins.then_inc(s["yn_t"], 1)

            def xn_t(b, i):
                pe.wait_ge(s["xn_ready"], b + 1)
                for k in range(2):
                    ins = pe.transpose(t1_bank[:, k * P:(k + 1) * P], xn[:, i, k * P:(k + 1) * P], ident[:, :])
                ins.then_inc(s["xn_t"], 1)

            def yw(b, i):
                pe.wait_ge(s["xnt_copied"], b + 1)
                for k in range(2):
                    ins = pe.matmul(t1_bank[:, 0:D + NE], xnt[:, i, k, :], wr_moving[:, k, :],
                                    start=(k == 0), stop=(k == 1))
                ins.then_inc(s["yw_ready"], 1)

            pe.wait_ge(s["ident_done"], 1)
            pe.wait_ge(s["ones_done"], 1)
            ctx_t(0)
            pe.wait_ge(s["vt_done"], 1)
            ctx_t(1)
            pe.wait_ge(s["stacks_loaded"], 96)
            scores(0, 0, 0, 0, None)
            scores(1, 0, 0, 1, None)
            for step in range(2, STEPS):
                scores(step, 0, step // NH, step % NH, step - 1)
                if step == NH + 1:
                    pe.wait_ge(s["vt_done"], 2)
                    max_t(0, 0)
            pe.wait_ge(s["w_ones"], 16)
            scores_t(0, 0, 0, False)
            scores_t(1, 0, 1, False)

            def unit(u, first, second, last, vt_left=True):
                for j in range(STEPS):
                    if j < STEPS - 2:
                        scores_t(STEPS * u + j + 2, u, j + 2, True)
                    elif not last:
                        scores_t(STEPS * (u + 1) + j - 14, u + 1, j - 14, True)
                    if not last:
                        if j == 0:
                            pe.wait_ge(s["stacks_loaded"], 96 * (u + 2))
                        scores(STEPS * (u + 1) + j, u + 1, j // NH, j % NH, STEPS * (u + 1) + j - 1)
                    values(STEPS * u + j, 2 * u + j // NH, j, first)
                    if j == 0:
                        pe.wait_ge(s["neg_done"], 2 * u + 1)
                        max_t(2 * u + 1, 1)
                    if j == 1 and not first:
                        if not second:
                            pe.wait_ge(s["yw_done"], 2 * u - 2)
                        yn_t(2 * u - 2, 0)
                    if j == 3 and not first:
                        pe.wait_ge(s["x1_done"], 2 * (2 * u - 2) + 1)
                        yn_t(2 * u - 1, 1)
                    if j == 5 and vt_left:
                        pe.wait_ge(s["neg_done"], 2 * u + 2)
                        ctx_t(u + 2)
                    if j == 9 and not last:
                        if vt_left:
                            pe.wait_ge(s["vt_done"], u + 3)
                        else:
                            pe.wait_ge(s["neg_done"], 2 * u + 2)
                        max_t(2 * u + 2, 0)
                    if j == 10 and not first:
                        pe.wait_ge(s["x1_done"], 2 * (2 * u - 1) + 1)
                        xn_t(2 * u - 2, 0)
                    if j == 12 and not first:
                        pe.wait_ge(s["xnt_copied"], 2 * u - 1)
                        xn_t(2 * u - 1, 1)
                    if j == 13 and not first:
                        if second:
                            pe.wait_ge(s["w_small"], 16 * 10)
                        pe.wait_ge(s["xnt_copied"], 2 * u)
                        yw(2 * u - 2, 0)
                    if j == 15 and not first:
                        pe.wait_ge(s["yw_done"], 2 * u - 1)
                        yw(2 * u - 1, 1)

            unit(0, True, False, False)
            unit(1, False, True, False)
            with pe.Fori(2, NU - 2) as u:
                unit(u, False, False, False)
            unit(NU - 2, False, False, False, False)
            unit(NU - 1, False, False, True, False)
            b = NB - 2
            pe.wait_ge(s["yw_done"], b)
            yn_t(b, 0)
            pe.wait_ge(s["x1_done"], 2 * b + 1)
            yn_t(b + 1, 1)
            pe.wait_ge(s["x1_done"], 2 * b + 3)
            xn_t(b, 0)
            pe.wait_ge(s["xnt_copied"], b + 1)
            xn_t(b + 1, 1)
            pe.wait_ge(s["xnt_copied"], b + 2)
            yw(b, 0)
            pe.wait_ge(s["yw_done"], b + 1)
            yw(b + 1, 1)

            pe.wait_ge(s["sh_exp"], 3)
            for g in range(2):
                ins = pe.transpose(t0_bank[:, g * P:(g + 1) * P],
                                   logits[:, NH * g:NH * (g + 1), :].rearrange("p b e -> p (b e)"), ident[:, :])
            ins.then_inc(s["st_t"], 1)
            with pe.Fori(0, SEARCH_BITS) as n:
                pe.wait_ge(s["counted"], n + 1)
                pe.matmul(t1_bank[:, 0:1], same_expert[:, :], count[:, :], start=True, stop=True).then_inc(s["totalled"], 1)
            pe.wait_ge(s["counted"], SEARCH_BITS + 1)
            pe.matmul(t1_bank[:, 1:2], same_expert[:, :], count[:, :], start=True, stop=True).then_inc(s["gt_total"], 1)
            pe.wait_ge(s["eq_counted"], 1)
            pe.matmul(t1_bank[:, 2:4], earlier_batch[:, :], totals[:, :], start=True, stop=True)
            pe.matmul(t1_bank[:, 4:5], same_expert[:, :], totals[:, 0:1], start=True, stop=True).then_inc(s["eq_total"], 1)
            pe.wait_ge(s["gated_ready"], 1)
            for g in range(2):
                ins = pe.matmul(t0_bank[:, NH * g:NH * (g + 1)], gated[:, g, :], batch_of[:, :], start=True, stop=True)
            ins.then_inc(s["gate_t"], 1)

            def pair(v, c, d, first):
                if c:
                    for i in range(2):
                        b = 2 * v + i
                        pe.wait_ge(s["c_xn"], 3 * b + 3)
                        if not first:
                            pe.wait_ge(s["c_x3"], b - 1)
                        for k in range(2):
                            ins = pe.transpose(c_bank[i][:, k * P:(k + 1) * P], xn[:, i, k * P:(k + 1) * P], ident[:, :])
                        ins.then_inc(s["c_xn_t"], 1)
                    for i in range(2):
                        b = 2 * v + i
                        pe.wait_ge(s["c_xnt"], b + 1)
                        for k in range(2):
                            pe.matmul(c_bank[i][:, 256:384], xnt[:, i, k, :], vt[:, b, k, :, 0:C],
                                      start=(k == 0), stop=False)
                        ins = pe.matmul(c_bank[i][:, 256:384], ones[0:1, :], mask_bias[:, b, :], start=False, stop=True)
                        ins.then_inc(s["c_scores"], 1)
                if d:
                    for i in range(2):
                        b = 2 * v - 2 + i
                        pe.wait_ge(s["d_score"], b + 1)
                        if not (isinstance(b, int) and b < 2):
                            pe.wait_ge(s["d_zg"], b - 1)
                        pe.transpose(d_bank[i][:, 0:P], score[:, i:i + 1].to_broadcast([P, P]), ident[:, :]).then_inc(s["d_row"], 1)
                if c:
                    for i in range(2):
                        pe.wait_ge(s["c_exp"], 2 * v + i + 1)
                        pe.transpose(c_bank[i][:, 384:512], attn[:, i, :], ident[:, :]).then_inc(s["c_attn_t"], 1)
                    for i in range(2):
                        b = 2 * v + i
                        pe.wait_ge(s["c_attnt"], b + 1)
                        pe.matmul(c_bank[i][:, 0:D], attn_t[:, i, :], ctx[:, b, :], start=True, stop=True).then_inc(s["c_read"], 1)
                if d:
                    for i in range(2):
                        b = 2 * v - 2 + i
                        pe.wait_ge(s["d_pick"], b + 1)
                        for k in range(2):
                            ins = pe.matmul(d_bank[i][:, P + k * KT:P + (k + 1) * KT], z[:, i, k * P:(k + 1) * P],
                                            pick[:, i, :], start=True, stop=True)
                        ins.then_inc(s["d_gath"], 1)

            pair(0, True, False, True)
            pair(1, True, True, False)
            with pe.Fori(2, NU) as v:
                pair(v, True, True, False)
            pair(NU, False, True, False)

            pe.wait_ge(s["w_big"], 16 * 3)
            pe.wait_ge(s["d_zg"], NB)
            pe.wait_ge(s["d_pickbf"], NB)

            def group(g, first):
                for t in range(2):
                    if not (first and t == 0):
                        pe.wait_ge(s["f_ptc"], 2 * g + t)
                    pe.transpose(pick_t_psum, pick_bf[:, bass.ds(4 * g + 2 * t, 2), :].rearrange("p b k -> p (b k)"),
                                 ident_bf[:, :]).then_inc(s["f_pt"], 1)
                for f in range(NF):
                    if not (first and f < 2):
                        pe.wait_ge(s["f_gelu"], NF * g + max(f - 1, 0))
                    for k in range(2):
                        ins = pe.matmul(hid_bank[f % 2][:, 0:4 * KT], w1s[:, k, f * P:(f + 1) * P],
                                        zg[:, k, bass.ds(4 * KT * g, 4 * KT)], start=(k == 0), stop=(k == 1))
                    ins.then_inc(s["f_h"], 1)
                pe.wait_ge(s["f_gelu"], NF * (g + 1))
                if not first:
                    pe.wait_ge(s["f_taken"], 2 * g)
                for t in range(2):
                    for f in range(NF):
                        ins = pe.matmul(y_bank[t][:, 0:D], hid[:, f, t * P:(t + 1) * P], w2s[:, f, :],
                                        start=(f == 0), stop=(f == NF - 1))
                    ins.then_inc(s["f_y"], 1)
                for t in range(2):
                    pe.wait_ge(s["f_taken"], 2 * g + t + 1)
                    pe.wait_ge(s["f_ptc"], 2 * g + t + 1)
                    for i in range(2):
                        if not (first and t == 0):
                            pe.wait_ge(s["f_out"], 4 * g + (0 if t == 0 else 1 + i))
                        pe.matmul(put_bank[i][:, 0:D], pick_t[i * KT:(i + 1) * KT, t, :],
                                  taken_out[i * KT:(i + 1) * KT, t, :], start=True, stop=True).then_inc(s["f_sc"], 1)

            group(0, True)
            with pe.Fori(1, NG) as g:
                group(g, False)


_INS = ['x', 'ctx_2048', 'mask_BxS2_bk0', 'L0_ffn_router_w', 'L0_ffn_router_b', 'L0_ffn_expert_w',
        'L0_ffn_expert_b', 'L1_ffn_w_r', 'L1_ffn_b_r', 'L1_ffn_w1', 'L1_ffn_b1', 'L1_ffn_w2', 'L1_ffn_b2']
_OUTS = [((16, 128, 256), 'float32')]


def kernel(**inputs):
    import numpy as _np
    import concourse.bacc as _bacc
    from concourse import mybir as _mybir
    from concourse.bass_utils import run_bass_kernel_spmd as _run

    nc = _bacc.Bacc("TRN2", target_bir_lowering=False, num_devices=1)
    arrays, args = {}, []
    for name in _INS:
        a = _np.ascontiguousarray(inputs[name])
        if a.ndim == 0:
            a = a.reshape(1)
        arrays[f"in_{name}_dram"] = a
        args.append(nc.dram_tensor(f"in_{name}_dram", a.shape, _mybir.dt.from_np(a.dtype), kind="ExternalInput").ap())
    for i, (shape, dtype) in enumerate(_OUTS):
        dt = _mybir.dt.from_np(_np.dtype(dtype))
        args.append(nc.dram_tensor(f"out_{i}_dram", shape, dt, kind="ExternalOutput").ap())
    build_program(nc, *args)
    r = _run(nc, [arrays], core_ids=[0])
    return r.results[0]["out_0_dram"]
```

```python
from contextlib import ExitStack

import concourse.bass as bass
from concourse import mybir

F32 = mybir.dt.float32
BF16 = mybir.dt.bfloat16
I32 = mybir.dt.int32
U8 = mybir.dt.uint8
ALU = mybir.AluOpType
ACT = mybir.ActivationFunctionType
AX = mybir.AxisListType

P = 128
NB = 16
D = 256
NH = 8
C = P // NH
Q = 32
NU = NB // 2
STEPS = 2 * NH
NE = 16
KE = NB * P // NE
KT = P // 2
DF = 4 * D
NF = DF // P
NG = 4
EPS = 1e-5
MASKED = -1e30
SLOTS = 3
QROWS = 6 * C
SROWS = QROWS + 2
BITS_A_TURN = 5
SEARCH_BITS = 30


def build_program(nc, x, ctx_2048, mask, router_w, router_b, expert_w, expert_b,
                  w_r, b_r, w1, b1, w2, b2, out):
    with ExitStack() as stack:
        def sb(name, shape, dt=F32):
            return stack.enter_context(nc.sbuf_tensor(name, shape, dt))

        def bank(name):
            return stack.enter_context(nc.psum_tensor(name, [P, 512], F32))

        def sem(name):
            return stack.enter_context(nc.semaphore(name))

        q_parts_dram = nc.dram_tensor("q_parts_dram", (NU, 3, C, NH, 2 * D), BF16, kind="Internal").ap()
        k_parts_dram = nc.dram_tensor("k_parts_dram", (NU, 3, C, NH, 2 * D), BF16, kind="Internal").ap()

        xs = sb("xs", [P, NB, D])
        ctx = sb("ctx", [P, NB, D])
        ctx_stage = sb("ctx_stage", [P, 2, D])
        x_stage = sb("x_stage", [P, 2, D])
        x_new = sb("x_new", [P, 2, D])
        x_new3 = sb("x_new3", [P, 2, D])
        vt = sb("vt", [P, NB, 2, P])
        values_ones = sb("values_ones", [P, 2, 2, NH // 2, 2, Q])
        y = sb("y", [P, NB, D])
        q_stack = sb("q_stack", [P, SLOTS, NH, 2, D], BF16)
        k_stack = sb("k_stack", [P, SLOTS, NH, 2, D], BF16)
        probs = sb("probs", [P, 4, 512])
        mv0 = sb("mv0", [P, 2, 2])
        st = sb("st", [P, 2, 6])
        var16 = sb("var16", [P, 2])
        rstd_q = sb("rstd_q", [P, 2])
        minus_half = sb("minus_half", [P, 2])
        qn = sb("qn", [P, 2, D])
        q_rest = sb("q_rest", [P, 2 * D])
        q_parts = sb("q_parts", [P, 3, 2 * D], BF16)
        k_rest = sb("k_rest", [P, 2 * D])
        k_parts = sb("k_parts", [P, 3, 2 * D], BF16)
        row_max = sb("row_max", [P, 2, 2, NH])
        neg_max = sb("neg_max", [NH, 2, 2, D], BF16)
        low = sb("low", [P, 1])
        high = sb("high", [P, 1])
        num_low = sb("num_low", [P, 2, D])
        sum_high = sb("sum_high", [P, 2, D])
        numer = sb("numer", [P, 2, D])
        denom = sb("denom", [P, 2, D])
        denom_inv = sb("denom_inv", [P, 2, D])
        denom_own = sb("denom_own", [P, 2, D])
        mv = sb("mv", [P, 2, 2])
        var_eps = sb("var_eps", [P, 2])
        rstd = sb("rstd", [P, 2])
        xn = sb("xn", [P, 2, D])
        xnt = sb("xnt", [P, 2, 2, P])
        wr_moving = sb("wr_moving", [P, 2, D + NE])
        eb_rows = sb("eb_rows", [P, D + NE])
        logits = sb("logits", [P, NB, NE])
        lg_max = sb("lg_max", [P, NB])
        lg_sum = sb("lg_sum", [P, NB])
        lg_inv = sb("lg_inv", [P, NB])
        st_probs = sb("st_probs", [P, 2, P])
        ident = sb("ident", [P, P])
        ident_bf = sb("ident_bf", [P, P], BF16)
        earlier = sb("earlier", [P, P])
        same_expert = sb("same_expert", [P, P], BF16)
        earlier_batch = sb("earlier_batch", [P, P], BF16)
        batch_of = sb("batch_of", [P, NH])
        free_i = sb("free_i", [P, P], I32)
        part_i = sb("part_i", [P, 1], I32)
        work_i = sb("work_i", [P, P], I32)
        work_p = sb("work_p", [P, 2], I32)
        half_i = sb("half_i", [P, 1], I32)
        free_f = sb("free_f", [P, P])
        part_f = sb("part_f", [P, 1])
        free_lo = sb("free_lo", [P, P])
        free_hi = sb("free_hi", [P, P])
        part_lo = sb("part_lo", [P, 1])
        part_hi = sb("part_hi", [P, 1])
        ones = sb("ones", [P, P])
        ones_bf = sb("ones_bf", [2, 2 * D], BF16)
        junk = sb("junk", [P, 2, P])
        bits = sb("bits", [P, 2], I32)
        thr = sb("thr", [P, 1], I32)
        cand = sb("cand", [P, 1], I32)
        taken = sb("taken", [P, 1], I32)
        count = sb("count", [P, 1], BF16)
        above = sb("above", [P, 2, P])
        equal = sb("equal", [P, 2, P])
        running = sb("running", [P, 2, P])
        totals = sb("totals", [P, 2], BF16)
        base = sb("base", [P, 2])
        need = sb("need", [P, 1])
        gated = sb("gated", [P, 2, P])
        gate = sb("gate", [P, NB])
        mask_u8 = sb("mask_u8", [P, NB, P], U8)
        mask_bias = sb("mask_bias", [1, NB, P], BF16)
        valid = sb("valid", [P, NB])
        sc_max = sb("sc_max", [P, 2])
        sc_bias = sb("sc_bias", [P, 2])
        sc_sum = sb("sc_sum", [P, 2])
        sc_inv = sb("sc_inv", [P, 2])
        sc_coef = sb("sc_coef", [P, 2])
        attn = sb("attn", [P, 2, P])
        attn_t = sb("attn_t", [P, 2, P])
        st3 = sb("st3", [P, 2, 6])
        mv3 = sb("mv3", [P, 2, 2])
        var_eps3 = sb("var_eps3", [P, 2])
        rstd3 = sb("rstd3", [P, 2])
        z = sb("z", [P, 2, D])
        z_work = sb("z_work", [P, 2, D])
        wr_rows = sb("wr_rows", [P, D])
        br_rows = sb("br_rows", [P, 1])
        score0 = sb("score0", [P, 2])
        score = sb("score", [P, 2])
        rank_gt = sb("rank_gt", [P, 2])
        rank_eq = sb("rank_eq", [P, 2])
        rank = sb("rank", [P, 2])
        cmp_work = sb("cmp_work", [P, 2, P])
        pick = sb("pick", [P, 2, KT])
        pick_bf = sb("pick_bf", [P, NB, KT], BF16)
        zg = q_stack[:, 0].rearrange("p h b n -> p (h b n)").bitcast(F32).rearrange("p (k t) -> p k t", k=2)
        w1s = k_stack[:, 0].rearrange("p h b n -> p (h b n)").bitcast(F32).rearrange("p (k f) -> p k f", k=2)
        w2s = k_stack[:, 1].rearrange("p h b n -> p (h b n)").bitcast(F32).rearrange("p (k n) -> p k n", k=NF)
        b1s = sb("b1s", [P, NF])
        b2_rows = sb("b2_rows", [P, D])
        hid = probs[:, 0:2, :].rearrange("p s (f t) -> p (s f) t", f=4)
        taken_out = sb("taken_out", [P, D])
        pick_t = sb("pick_t", [P, P])
        out_rows = y

        score_bank = [bank("score_bank0"), bank("score_bank1")]
        scoret_bank = [bank("scoret_bank0"), bank("scoret_bank1")]
        pv_bank = [bank("pv_bank0"), bank("pv_bank1")]
        t0_bank = bank("t0_bank")
        t1_bank = bank("t1_bank")

        c_bank, d_bank = score_bank, scoret_bank
        hid_bank, y_bank, put_bank = pv_bank, t0_bank, [t1_bank, t0_bank]
        pick_t_psum = t1_bank[:, 0:P // 2].bitcast(BF16)

        names = """passed kept w_ones x_loaded ctx_loaded staged parts_written stacks_loaded w_small w_big consts_dma
        iota_done ident_done consts_done ones_done k_high k_rest k_mid k_split q_ready q_high q_rest q_mid q_split stats_q var_q root_q
        var1 root1 values_ready even_taken div_step bn1
        scores_ready max_done scorest_ready exp_done pv_done max_t ctx_t vt_done neg_hi neg_done
        x1_done stats1 xn_ready xn_t xnt_copied yw_ready yw_done
        bn_q sh_exp st_t st_copied cand_ready counted totalled gt_counted gt_total eq_counted eq_total gated_ready gate_t gate_done
        c_bn c_stats c_var c_root c_xn c_xn_t c_xnt c_scores c_max c_bias c_exp c_attn_t c_attnt c_coef c_read c_x3
        d_bn d_stats d_var d_root d_z d_dot d_score d_rank d_row d_pick d_pickbf d_gath d_zg
        f_h f_gelu f_y f_taken f_pt f_ptc f_sc f_out out_stored""".split()
        s = {n: sem("s_" + n) for n in names}
        neg_loaded = [sem("s_neg_loaded0"), sem("s_neg_loaded1")]

        block = stack.enter_context(nc.Block())

        def is_first(u):
            return isinstance(u, int) and u == 0

        def is_n(u, n):
            return isinstance(u, int) and u == n

        def wait_apart(eng, semaphore, value):
            eng.wait_ge(semaphore, value)
            eng.sem_inc(s["passed"], 1)

        @block.sync
        def _(sp):
            x_rows = x.rearrange("b c n -> c b n")
            ctx_rows = ctx_2048.rearrange("b c n -> c b n")

            def load_stage(u):
                if not is_first(u):
                    sp.wait_ge(s["ctx_t"], u)
                    sp.wait_ge(s["k_split"], u)
                    sp.wait_ge(s["q_split"], u)
                sp.dma_start(ctx_stage[:, :, :], ctx_rows[:, bass.ds(2 * u, 2), :]).then_inc(s["staged"], 16)
                sp.dma_start(x_stage[:, :, :], x_rows[:, bass.ds(2 * u, 2), :]).then_inc(s["staged"], 16)

            def write_k_parts(u):
                sp.wait_ge(s["k_split"], u + 1)
                for part in range(3):
                    sp.dma_start(k_parts_dram[u, part].rearrange("d h n -> h d n"),
                                 k_parts[:, part, :]).then_inc(s["parts_written"], 16)

            def write_q_parts(u):
                sp.wait_ge(s["q_split"], u + 1)
                for part in range(3):
                    sp.dma_start(q_parts_dram[u, part].rearrange("d h n -> h d n"),
                                 q_parts[:, part, :]).then_inc(s["parts_written"], 16)

            def load_stacks(u, reused):
                slot = u % SLOTS
                wait_apart(sp, s["parts_written"], 96 * (u + 1))
                if not is_first(u):
                    wait_apart(sp, s["stacks_loaded"], 96 * u)
                if reused:
                    wait_apart(sp, s["scorest_ready"], STEPS * (u - SLOTS + 1))
                k_rows = k_parts_dram[u].rearrange("p d h n -> (p d) (h n)")
                q_rows = q_parts_dram[u].rearrange("p d h n -> p d (h n)")
                k_to = k_stack[:, slot].rearrange("p h b n -> p (h b n)")
                q_to = q_stack[:, slot].rearrange("p h b n -> p (h b n)")
                n = NH * 2 * D
                sp.dma_start(k_to[0:3 * C], k_rows).then_inc(s["stacks_loaded"], 16)
                sp.dma_start(k_to[3 * C:5 * C], k_rows[0:2 * C]).then_inc(s["stacks_loaded"], 16)
                sp.dma_start(k_to[5 * C:6 * C], k_rows[0:C]).then_inc(s["stacks_loaded"], 16)
                sp.dma_start(q_to[0:3 * C], q_rows[0:1].to_broadcast([3, C, n])).then_inc(s["stacks_loaded"], 16)
                sp.dma_start(q_to[3 * C:5 * C], q_rows[1:2].to_broadcast([2, C, n])).then_inc(s["stacks_loaded"], 16)
                sp.dma_start(q_to[5 * C:6 * C], q_rows[2]).then_inc(s["stacks_loaded"], 16)

            def load_neg_max(u, i):
                wait_apart(sp, s["neg_done"], 2 * u + i + 1)
                for part in range(2):
                    sp.dma_start(q_stack[QROWS + part:QROWS + part + 1, u % SLOTS, :, i, :],
                                 neg_max[:, i, part, :]).then_inc(neg_loaded[i], 16)

            load_stage(0)
            sp.wait_ge(s["ones_done"], 1)
            sp.dma_start(k_stack[QROWS:SROWS].rearrange("p s h b n -> p (s h) (b n)"),
                         ones_bf[:, :].unsqueeze(1).to_broadcast([2, SLOTS * NH, 2 * D])).then_inc(s["w_ones"], 16)
            sp.dma_start(xs[:, :, :], x_rows).then_inc(s["x_loaded"], 16)
            sp.dma_start(ctx[:, :, :], ctx_rows).then_inc(s["ctx_loaded"], 16)
            for half in range(2):
                sp.dma_start(wr_moving[:, half, 0:D], expert_w[half * P:(half + 1) * P, :]).then_inc(s["w_small"], 16)
                sp.dma_start(wr_moving[:, half, D:D + NE], router_w[half * P:(half + 1) * P, :]).then_inc(s["w_small"], 16)
            for dst, row in ((eb_rows[:, 0:D], expert_b), (eb_rows[:, D:D + NE], router_b),
                             (wr_rows[:, :], w_r), (b2_rows[:, :], b2)):
                sp.dma_start(dst, row.rearrange("(a n) -> a n", a=1).to_broadcast([P, row.shape[0]])).then_inc(s["w_small"], 16)
            sp.dma_start(br_rows[:, :], b_r.to_broadcast([P, 1])).then_inc(s["w_small"], 16)
            sp.dma_start(mask_u8[:, :, :], mask.rearrange("(a b) m -> a b m", a=1).to_broadcast([P, NB, P])).then_inc(s["w_small"], 16)
            write_k_parts(0)
            write_q_parts(0)
            load_stage(1)
            load_stacks(0, False)
            write_k_parts(1)
            write_q_parts(1)
            load_stage(2)
            load_stacks(1, False)
            load_neg_max(0, 0)
            with nc.allow_non_contiguous_dma(reason="1024 single biases, one per partition and block"):
                sp.dma_start(b1s[:, :], b1.rearrange("(k p) -> p k", p=P)).then_inc(s["w_big"], 16)

            def unit(u, more_stage, more_parts, more_max, reused):
                load_neg_max(u, 1)
                if more_parts:
                    write_k_parts(u + 2)
                    write_q_parts(u + 2)
                    if more_stage:
                        load_stage(u + 3)
                    load_stacks(u + 2, reused)
                if more_max:
                    load_neg_max(u + 1, 0)

            unit(0, True, True, True, False)
            unit(1, True, True, True, True)
            with sp.Fori(2, NU - 3) as u:
                unit(u, True, True, True, True)
            unit(NU - 3, False, True, True, True)
            unit(NU - 2, False, False, True, True)
            unit(NU - 1, False, False, False, True)
            sp.wait_ge(s["scorest_ready"], STEPS * NU)
            sp.dma_start(w1s, w1.rearrange("(k p) f -> p k f", p=P)).then_inc(s["w_big"], 16)
            sp.dma_start(w2s, w2.rearrange("(k p) f -> p k f", p=P)).then_inc(s["w_big"], 16)

            def store(t):
                sp.wait_ge(s["f_out"], 2 * t + 2)
                sp.dma_start(out.rearrange("b t n -> t b n")[:, bass.ds(2 * t, 2), :],
                             out_rows[:, bass.ds(2 * t, 2), :]).then_inc(s["out_stored"], 16)

            with sp.Fori(0, NU) as t:
                store(t)
            sp.wait_ge(s["out_stored"], 16 * NU)

        @block.gpsimd
        def _(pool):
            pool.iota(free_i[:, :], pattern=[[1, P]], base=0, channel_multiplier=0).then_inc(s["iota_done"], 1)
            pool.wait_ge(s["iota_done"], 1)
            pool.iota(part_i[:, :], pattern=[[0, 1]], base=0, channel_multiplier=1).then_inc(s["iota_done"], 1)
            pool.wait_ge(s["ones_done"], 1)

            def rest_k(u):
                wait_apart(pool, s["k_high"], u + 1)
                pool.tensor_tensor(k_rest[:, :], ctx_stage[:, :, :].rearrange("p b n -> p (b n)"), k_parts[:, 0, :],
                                   ALU.subtract).then_inc(s["k_rest"], 1)

            def low_k(u):
                wait_apart(pool, s["k_mid"], u + 1)
                pool.tensor_tensor(k_parts[:, 2, :], k_rest[:, :], k_parts[:, 1, :], ALU.subtract).then_inc(s["k_split"], 1)

            def rest_q(u):
                wait_apart(pool, s["q_high"], u + 1)
                pool.tensor_tensor(q_rest[:, :], qn[:, :, :].rearrange("p b n -> p (b n)"), q_parts[:, 0, :],
                                   ALU.subtract).then_inc(s["q_rest"], 1)

            def low_q(u):
                wait_apart(pool, s["q_mid"], u + 1)
                pool.tensor_tensor(q_parts[:, 2, :], q_rest[:, :], q_parts[:, 1, :], ALU.subtract).then_inc(s["q_split"], 1)

            def inverse_root(dst, variance, work, factor, known, summed, ready, n):
                wait_apart(pool, s[known], n + 1)
                pool.tensor_scalar(work, variance, EPS, factor, ALU.add, ALU.mult).then_inc(s[summed], 1)
                wait_apart(pool, s[summed], n + 1)
                pool.tensor_tensor(dst, work, minus_half[:, 0:dst.shape[1]], ALU.pow).then_inc(s[ready], 1)

            def root_q(u):
                inverse_root(rstd_q[:, :], mv0[:, :, 1], var16[:, :], float(C), "stats_q", "var_q", "root_q", u)

            def root_rows(b, i):
                inverse_root(rstd[:, i:i + 1], mv[:, i, 1:2], var_eps[:, i:i + 1], 1.0, "stats1", "var1", "root1", b)

            def keep_rows(rows, b, i):
                pool.tensor_copy(xs[:, b, :], rows[:, i, :]).then_inc(s["kept"], 1)

            def fill_values(b, u, i, first):
                if not first:
                    pool.wait_ge(s["pv_done"], NH * (b - 1))
                wait_apart(pool, s["vt_done"], u + 1)
                for odd in range(2):
                    from_ = vt[:, b, :, :].rearrange("p k (q o c) -> p k q o c", q=NH // 2, o=2)[:, :, :, odd, :]
                    ins = pool.tensor_copy(values_ones[:, i, :, :, odd, odd * C:odd * C + C], from_)
                ins.then_inc(s["values_ready"], 1)

            for u in range(2):
                root_q(u)
                rest_k(u)
                low_k(u)
                rest_q(u)
                low_q(u)
            fill_values(0, 0, 0, True)
            rest_k(2)
            root_q(2)

            def unit(u, first, parts, more_parts, last):
                if parts:
                    low_k(u + 2)
                    rest_q(u + 2)
                fill_values(2 * u + 1, u, 1, first)
                if parts:
                    low_q(u + 2)
                if not first:
                    root_rows(2 * u - 1, 1)
                    keep_rows(x_new, 2 * u - 1, 1)
                if not last:
                    fill_values(2 * u + 2, u + 1, 0, False)
                root_rows(2 * u, 0)
                keep_rows(x_new, 2 * u, 0)
                if more_parts:
                    rest_k(u + 3)
                    root_q(u + 3)

            unit(0, True, True, True, False)
            with pool.Fori(1, NU - 3) as u:
                unit(u, False, True, True, False)
            unit(NU - 3, False, True, False, False)
            unit(NU - 2, False, False, False, False)
            unit(NU - 1, False, False, False, True)
            root_rows(NB - 1, 1)
            keep_rows(x_new, NB - 1, 1)

            def c_roots(t):
                for i in range(2):
                    inverse_root(rstd[:, i:i + 1], mv[:, i, 1:2], var_eps[:, i:i + 1], 1.0,
                                 "c_stats", "c_var", "c_root", 2 * t + i)

            def turn(v, c, d, more_c):
                if d:
                    for i in range(2):
                        b = 2 * v - 2 + i
                        wait_apart(pool, s["d_pick"], b + 1)
                        pool.tensor_copy(pick_bf[:, b, :], pick[:, i, :]).then_inc(s["d_pickbf"], 1)
                if more_c:
                    c_roots(v + 1)
                if c:
                    for i in range(2):
                        inverse_root(rstd3[:, i:i + 1], mv3[:, i, 1:2], var_eps3[:, i:i + 1], 1.0,
                                     "d_stats", "d_var", "d_root", 2 * v + i)
                    for i in range(2):
                        keep_rows(x_new3, 2 * v + i, i)

            c_roots(0)
            turn(0, True, False, True)
            with pool.Fori(1, NU - 1) as v:
                turn(v, True, True, True)
            turn(NU - 1, True, True, False)
            turn(NU, False, True, False)

        @block.vector
        def _(dve):
            dve.memset(minus_half[:, :], -0.5)
            dve.memset(values_ones[:, :, :, :, :, :], 1.0)
            dve.memset(ones[:, :], 1.0)
            dve.memset(ones_bf[:, :], 1.0).then_inc(s["ones_done"], 1)
            dve.wait_ge(s["iota_done"], 2)
            k = [0]

            def link(ins):
                k[0] += 1
                ins.then_inc(s["consts_done"], 1)
                dve.wait_ge(s["consts_done"], k[0])

            dve.tensor_copy(free_f[:, :], free_i[:, :])
            link(dve.tensor_copy(part_f[:, :], part_i[:, :]))
            dve.tensor_scalar(ident[:, :], free_f[:, :], part_f[:, 0:1], None, ALU.is_equal).then_inc(s["ident_done"], 1)
            dve.wait_ge(s["ident_done"], 1)

            def stats_q(u):
                if not is_first(u):
                    dve.wait_ge(s["q_split"], u)
                dve.wait_ge(s["staged"], 32 * (u + 1))
                for i in range(2):
                    dve.bn_stats(st[:, i, :], x_stage[:, i, :]).then_inc(s["bn_q"], 1)
                wait_apart(dve, s["bn_q"], 2 * u + 2)
                dve.bn_aggr(mv0[:, 0, :], st[:, 0, :])
                dve.bn_aggr(mv0[:, 1, :], st[:, 1, :]).then_inc(s["stats_q"], 1)

            stats_q(0)
            link(dve.tensor_scalar(earlier[:, :], free_f[:, :], part_f[:, 0:1], None, ALU.is_lt))
            dve.tensor_copy(ident_bf[:, :], ident[:, :])
            link(dve.tensor_scalar(work_i[:, :], free_i[:, :], 15, None, ALU.bitwise_and))
            link(dve.tensor_scalar(work_p[:, 0:1], part_i[:, :], 15, None, ALU.bitwise_and))
            link(dve.tensor_scalar(work_p[:, 1:2], part_i[:, :], 4, None, ALU.logical_shift_right))
            dve.tensor_copy(free_lo[:, :], work_i[:, :])
            dve.tensor_copy(part_lo[:, :], work_p[:, 0:1])
            link(dve.tensor_scalar(half_i[:, :], work_p[:, 1:2], 1, None, ALU.bitwise_and))
            link(dve.tensor_copy(high[:, :], half_i[:, :]))
            dve.tensor_scalar(low[:, :], high[:, :], -1.0, 1.0, ALU.mult, ALU.add)
            link(dve.tensor_copy(part_hi[:, :], work_p[:, 1:2]))
            link(dve.tensor_scalar(work_i[:, :], free_i[:, :], 4, None, ALU.logical_shift_right))
            link(dve.tensor_copy(free_hi[:, :], work_i[:, :]))
            dve.tensor_scalar(batch_of[:, :], free_f[:, 0:NH], part_hi[:, 0:1], None, ALU.is_equal)
            link(dve.tensor_scalar(same_expert[:, :], free_lo[:, :], part_lo[:, 0:1], None, ALU.is_equal))
            link(dve.scalar_tensor_tensor(earlier_batch[:, :], free_hi[:, :], part_hi[:, 0:1], same_expert[:, :],
                                          ALU.is_gt, ALU.mult))
            n_consts = k[0]

            def maximum(step, b, h, i, first_h):
                if first_h:
                    dve.wait_ge(s["max_t"], b - 1)
                dve.wait_ge(s["scores_ready"], step + 1)
                dve.tensor_reduce(row_max[:, i, :, h], score_bank[h % 2][:, :].rearrange("p (m n) -> p m n", m=2),
                                  AX.X, ALU.max).then_inc(s["max_done"], 1)

            def neg_low(b, i):
                dve.wait_ge(s["neg_hi"], b + 1)
                dve.scalar_tensor_tensor(neg_max[:, i, 1, :], t0_bank[0:NH, 0:D], -1.0, neg_max[:, i, 0, :],
                                         ALU.mult, ALU.subtract).then_inc(s["neg_done"], 1)

            def scale_q(u):
                dve.wait_ge(s["root_q"], u + 1)
                for i in range(2):
                    ins = dve.tensor_scalar(qn[:, i, :], x_stage[:, i, :], mv0[:, i, 0:1], rstd_q[:, i:i + 1],
                                            ALU.subtract, ALU.mult)
                ins.then_inc(s["q_ready"], 1)

            def gather_parts(b, i):
                odd_heads = pv_bank[i][:, D:2 * D]
                dve.wait_ge(s["even_taken"], b + 1)
                dve.scalar_tensor_tensor(denom[:, i, :], odd_heads, low[:, 0:1], sum_high[:, i, :],
                                         ALU.mult, ALU.add).then_inc(s["div_step"], 1)
                dve.scalar_tensor_tensor(numer[:, i, :], odd_heads, high[:, 0:1], num_low[:, i, :],
                                         ALU.mult, ALU.add).then_inc(s["div_step"], 1)

            def invert(b, i):
                dve.wait_ge(s["div_step"], 5 * b + 1)
                dve.reciprocal(denom_inv[:, i, :], denom[:, i, :]).then_inc(s["div_step"], 1)

            def bring_over(b, i):
                wait_apart(dve, s["div_step"], 5 * b + 3)
                dve.stream_shuffle(out=denom_own[:, i, :], in_=denom_inv[:, i, :],
                                   mask=[(n + C) % Q for n in range(Q)]).then_inc(s["div_step"], 1)
                dve.wait_ge(s["div_step"], 5 * b + 4)
                dve.tensor_tensor(numer[:, i, :], numer[:, i, :], denom_own[:, i, :], ALU.mult).then_inc(s["div_step"], 1)

            def add_x1(b, i, first):
                dve.wait_ge(s["div_step"], 5 * b + 5)
                if not first:
                    dve.wait_ge(s["kept"], b - 1)
                dve.tensor_tensor(x_new[:, i, :], numer[:, i, :], xs[:, b, :], ALU.add).then_inc(s["x1_done"], 1)
                dve.wait_ge(s["x1_done"], b + 1)
                dve.bn_stats(st3[:, i, :], x_new[:, i, :]).then_inc(s["bn1"], 1)
                wait_apart(dve, s["bn1"], b + 1)
                dve.bn_aggr(mv[:, i, :], st3[:, i, :]).then_inc(s["stats1"], 1)

            def scale_rows(b, i, first):
                if not first:
                    dve.wait_ge(s["xn_t"], b - 1)
                dve.wait_ge(s["root1"], b + 1)
                dve.tensor_scalar(xn[:, i, :], x_new[:, i, :], mv[:, i, 0:1], rstd[:, i:i + 1],
                                  ALU.subtract, ALU.mult).then_inc(s["xn_ready"], 1)

            def take_yw(b):
                dve.wait_ge(s["yw_ready"], b + 1)
                dve.tensor_tensor(y[:, b, :], t1_bank[:, 0:D], eb_rows[:, 0:D], ALU.add)
                dve.tensor_tensor(logits[:, b, :], t1_bank[:, D:D + NE], eb_rows[:, D:D + NE], ALU.add).then_inc(s["yw_done"], 1)

            def unit(u, first, second, last, parts, more_parts):
                a, b = 2 * u - 1, 2 * u
                for j in range(STEPS):
                    if not last:
                        maximum(STEPS * (u + 1) + j, 2 * (u + 1) + j // NH, j % NH, j // NH, j % NH == 0)
                    if j == 1 and parts:
                        scale_q(u + 2)
                    if j == 2:
                        neg_low(2 * u + 1, 1)
                    if j == 2 and not first:
                        gather_parts(a, 1)
                    if j == 3 and not first:
                        invert(a, 1)
                    if j == 4 and not first:
                        bring_over(a, 1)
                    if j == 5 and not first:
                        add_x1(a, 1, second)
                    if j == 6 and not first:
                        take_yw(2 * u - 2)
                    if j == 7 and not first:
                        scale_rows(a, 1, second)
                    if j == 10:
                        gather_parts(b, 0)
                    if j == 11 and not last:
                        neg_low(2 * u + 2, 0)
                    if j == 11:
                        invert(b, 0)
                    if j == 12:
                        bring_over(b, 0)
                    if j == 13:
                        add_x1(b, 0, first)
                    if j == 14 and not first:
                        take_yw(a)
                    if j == 15:
                        scale_rows(b, 0, first)
                    if j == 15 and more_parts:
                        stats_q(u + 3)

            scale_q(0)
            stats_q(1)
            scale_q(1)
            for j in range(2):
                maximum(j, 0, j, 0, False)
            with dve.Fori(1, NH // 2) as q:
                for j in range(2):
                    dve.wait_ge(s["scores_ready"], 2 * q + j + 1)
                    dve.tensor_reduce(row_max[:, 0, :, 2 * q + j],
                                      score_bank[j][:, :].rearrange("p (m n) -> p m n", m=2),
                                      AX.X, ALU.max).then_inc(s["max_done"], 1)
            neg_low(0, 0)
            with dve.Fori(0, NH // 2) as q:
                for j in range(2):
                    dve.wait_ge(s["scores_ready"], NH + 2 * q + j + 1)
                    dve.tensor_reduce(row_max[:, 1, :, 2 * q + j],
                                      score_bank[j][:, :].rearrange("p (m n) -> p m n", m=2),
                                      AX.X, ALU.max).then_inc(s["max_done"], 1)
            dve.wait_ge(s["w_small"], 16 * 10)
            dve.tensor_scalar(mask_bias[:, :, :], mask_u8[0:1, :, :], -1.0, -MASKED, ALU.add, ALU.mult)
            dve.tensor_reduce(valid[:, :], mask_u8[:, :, :], AX.X, ALU.max)
            dve.wait_ge(s["x_loaded"], 16)
            stats_q(2)
            unit(0, True, False, False, True, True)
            unit(1, False, True, False, True, True)
            with dve.Fori(2, NU - 3) as u:
                unit(u, False, False, False, True, True)
            unit(NU - 3, False, False, False, True, False)
            unit(NU - 2, False, False, False, False, False)
            unit(NU - 1, False, False, True, False, False)
            gather_parts(NB - 1, 1)
            invert(NB - 1, 1)
            bring_over(NB - 1, 1)
            add_x1(NB - 1, 1, False)
            take_yw(NB - 2)
            scale_rows(NB - 1, 1, False)
            take_yw(NB - 1)

            k[0] = n_consts
            dve.wait_ge(s["yw_done"], NB)
            link(dve.tensor_reduce(lg_max[:, :], logits[:, :, :], AX.X, ALU.max))
            dve.tensor_tensor(logits[:, :, :], logits[:, :, :], lg_max[:, :].unsqueeze(2).to_broadcast([P, NB, NE]),
                              ALU.subtract).then_inc(s["sh_exp"], 1)
            dve.wait_ge(s["sh_exp"], 2)
            link(dve.tensor_reduce(lg_sum[:, :], logits[:, :, :], AX.X, ALU.add))
            link(dve.reciprocal(lg_inv[:, :], lg_sum[:, :]))
            dve.tensor_tensor(logits[:, :, :], logits[:, :, :], lg_inv[:, :].unsqueeze(2).to_broadcast([P, NB, NE]),
                              ALU.mult).then_inc(s["sh_exp"], 1)
            link(dve.memset(thr[:, :], 0))
            dve.memset(cand[:, :], 1 << (SEARCH_BITS - 1))
            dve.memset(bits[:, 0:1], 1 << (SEARCH_BITS - 1))
            link(dve.memset(bits[:, 1:2], 1 << (SEARCH_BITS - 2)))
            dve.wait_ge(s["st_t"], 1)
            link(dve.tensor_copy(st_probs[:, :, :], t0_bank[:, 0:2 * P].rearrange("p (g t) -> p g t", g=2)))
            with dve.Fori(0, SEARCH_BITS // BITS_A_TURN) as turn:
                for n in (turn * BITS_A_TURN + r for r in range(BITS_A_TURN)):
                    dve.tensor_scalar(junk[:, :, :], st_probs[:, :, :], cand[:, :].bitcast(F32), None, ALU.is_ge, ALU.add,
                                      accum_out=count[:, :]).then_inc(s["counted"], 1)
                    dve.wait_ge(s["totalled"], n + 1)
                    dve.scalar_tensor_tensor(taken[:, :], t1_bank[:, 0:1], float(KE), bits[:, 0:1],
                                             ALU.is_ge, ALU.mult).then_inc(s["cand_ready"], 1)
                    dve.wait_ge(s["cand_ready"], 3 * n + 1)
                    dve.scalar_tensor_tensor(cand[:, :], taken[:, :], thr[:, 0:1], bits[:, 1:2],
                                             ALU.bitwise_or, ALU.bitwise_or).then_inc(s["cand_ready"], 1)
                    dve.wait_ge(s["cand_ready"], 3 * n + 2)
                    dve.tensor_tensor(thr[:, :], thr[:, :], taken[:, :], ALU.bitwise_or)
                    dve.tensor_scalar(bits[:, :], bits[:, :], 1, None, ALU.logical_shift_right).then_inc(s["cand_ready"], 1)
            dve.wait_ge(s["cand_ready"], 3 * SEARCH_BITS)
            threshold = thr[:, :].bitcast(F32)
            dve.tensor_scalar(above[:, :, :], st_probs[:, :, :], threshold, None, ALU.is_gt, ALU.add,
                              accum_out=count[:, :]).then_inc(s["counted"], 1)
            link(dve.tensor_scalar(equal[:, :, :], st_probs[:, :, :], threshold, None, ALU.is_equal))
            for g in range(2):
                link(dve.tensor_tensor_scan(running[:, g, :], ones[:, :], equal[:, g, :], 0.0, ALU.mult, ALU.add))
            dve.tensor_copy(totals[:, :], running[:, :, P - 1]).then_inc(s["eq_counted"], 1)
            dve.wait_ge(s["gt_total"], 1)
            dve.wait_ge(s["eq_total"], 1)
            link(dve.tensor_scalar(need[:, :], t1_bank[:, 1:2], -1.0, float(KE), ALU.mult, ALU.add))
            link(dve.tensor_copy(base[:, :], t1_bank[:, 2:4]))
            link(dve.tensor_tensor(base[:, 1:2], t1_bank[:, 4:5], base[:, 1:2], ALU.add))
            for g in range(2):
                link(dve.tensor_scalar(running[:, g, :], running[:, g, :], base[:, g:g + 1], need[:, 0:1], ALU.add, ALU.is_le))
            link(dve.tensor_tensor(equal[:, :, :], equal[:, :, :], running[:, :, :], ALU.mult))
            link(dve.tensor_tensor(above[:, :, :], above[:, :, :], equal[:, :, :], ALU.add))
            dve.tensor_tensor(gated[:, :, :], above[:, :, :], st_probs[:, :, :], ALU.mult).then_inc(s["gated_ready"], 1)
            dve.wait_ge(s["gate_t"], 1)
            link(dve.tensor_copy(gate[:, :], t0_bank[:, 0:NB]))

            def c_stats(b, i, first):
                if first:
                    dve.wait_ge(s["kept"], NB)
                else:
                    dve.wait_ge(s["c_x3"], b - 1)
                dve.scalar_tensor_tensor(x_new[:, i, :], y[:, b, :], gate[:, bass.ds(b, 1)], xs[:, b, :],
                                         ALU.mult, ALU.add).then_inc(s["c_bn"], 1)
                dve.wait_ge(s["c_bn"], 2 * b + 1)
                dve.bn_stats(st[:, i, :], x_new[:, i, :]).then_inc(s["c_bn"], 1)
                wait_apart(dve, s["c_bn"], 2 * b + 2)
                dve.bn_aggr(mv[:, i, :], st[:, i, :]).then_inc(s["c_stats"], 1)

            def c_scale(b, i, first):
                if not first:
                    dve.wait_ge(s["c_xn_t"], b - 1)
                dve.wait_ge(s["c_root"], b + 1)
                dve.tensor_scalar(xn[:, i, :], x_new[:, i, :], mv[:, i, 0:1], rstd[:, i:i + 1],
                                  ALU.subtract, ALU.mult).then_inc(s["c_xn"], 1)

            def d_scale(b, i, first):
                if not first:
                    dve.wait_ge(s["d_gath"], b - 1)
                dve.wait_ge(s["d_root"], b + 1)
                dve.tensor_scalar(z[:, i, :], x_new3[:, i, :], mv3[:, i, 0:1], rstd3[:, i:i + 1],
                                  ALU.subtract, ALU.mult).then_inc(s["d_z"], 1)

            def c_max(b, i):
                dve.wait_ge(s["c_scores"], b + 1)
                dve.tensor_reduce(sc_max[:, i:i + 1], c_bank[i][:, 256:384], AX.X, ALU.max).then_inc(s["c_max"], 1)
                dve.wait_ge(s["c_max"], b + 1)
                dve.tensor_scalar(sc_bias[:, i:i + 1], sc_max[:, i:i + 1], -(D ** -0.5), None,
                                  ALU.mult).then_inc(s["c_bias"], 1)

            def c_add(b, i, first):
                dve.wait_ge(s["c_exp"], b + 1)
                dve.reciprocal(sc_inv[:, i:i + 1], sc_sum[:, i:i + 1]).then_inc(s["c_coef"], 1)
                dve.wait_ge(s["c_coef"], 2 * b + 1)
                dve.tensor_tensor(sc_coef[:, i:i + 1], sc_inv[:, i:i + 1], valid[:, bass.ds(b, 1)],
                                  ALU.mult).then_inc(s["c_coef"], 1)
                dve.wait_ge(s["c_coef"], 2 * b + 2)
                dve.wait_ge(s["c_read"], b + 1)
                if not first:
                    dve.wait_ge(s["kept"], NB + b - 1)
                dve.scalar_tensor_tensor(x_new3[:, i, :], c_bank[i][:, 0:D], sc_coef[:, i:i + 1], x_new[:, i, :],
                                         ALU.mult, ALU.add).then_inc(s["c_x3"], 1)

            def d_stats(b, i):
                dve.wait_ge(s["c_x3"], b + 1)
                dve.bn_stats(st3[:, i, :], x_new3[:, i, :]).then_inc(s["d_bn"], 1)
                wait_apart(dve, s["d_bn"], b + 1)
                dve.bn_aggr(mv3[:, i, :], st3[:, i, :]).then_inc(s["d_stats"], 1)

            def d_score(b, i):
                dve.wait_ge(s["d_z"], b + 1)
                dve.tensor_tensor_reduce(out=z_work[:, i, :], in0=z[:, i, :], in1=wr_rows[:, :], scale=1.0, scalar=0.0,
                                         op0=ALU.mult, op1=ALU.add, accum_out=score0[:, i:i + 1]).then_inc(s["d_dot"], 1)
                dve.wait_ge(s["d_dot"], b + 1)
                dve.tensor_tensor(score[:, i:i + 1], score0[:, i:i + 1], br_rows[:, :], ALU.add).then_inc(s["d_score"], 1)

            def d_pick(b, i, first):
                row = d_bank[i][:, 0:P]
                dve.wait_ge(s["d_row"], b + 1)
                dve.tensor_scalar(cmp_work[:, i, :], row, score[:, i:i + 1], None, ALU.is_gt, ALU.add,
                                  accum_out=rank_gt[:, i:i + 1]).then_inc(s["d_rank"], 1)
                dve.wait_ge(s["d_rank"], 3 * b + 1)
                dve.scalar_tensor_tensor(cmp_work[:, i, :], row, score[:, i:i + 1], earlier[:, :], ALU.is_equal, ALU.mult,
                                         accum_out=rank_eq[:, i:i + 1]).then_inc(s["d_rank"], 1)
                dve.wait_ge(s["d_rank"], 3 * b + 2)
                dve.tensor_tensor(rank[:, i:i + 1], rank_gt[:, i:i + 1], rank_eq[:, i:i + 1], ALU.add).then_inc(s["d_rank"], 1)
                dve.wait_ge(s["d_rank"], 3 * b + 3)
                if not first:
                    dve.wait_ge(s["d_gath"], b - 1)
                    dve.wait_ge(s["d_pickbf"], b - 1)
                dve.tensor_scalar(pick[:, i, :], free_f[:, 0:KT], rank[:, i:i + 1], None, ALU.is_equal).then_inc(s["d_pick"], 1)

            def f_take(t, first):
                if not first:
                    dve.wait_ge(s["f_sc"], 2 * t)
                dve.wait_ge(s["f_y"], t + 1)
                dve.tensor_tensor(taken_out[:, :], y_bank[:, 0:D], b2_rows[:, :], ALU.add).then_inc(s["f_taken"], 1)

            def f_add(b, i):
                dve.wait_ge(s["kept"], NB + b + 1)
                dve.wait_ge(s["f_sc"], b + 1)
                dve.tensor_tensor(out_rows[:, b, :], put_bank[i][:, 0:D], xs[:, b, :],
                                  ALU.add).then_inc(s["f_out"], 1)

            def turn(v, c, d, f, o, more_c):
                for i in range(2):
                    if d:
                        d_scale(2 * v - 2 + i, i, is_n(v, 1))
                for i in range(2):
                    if d:
                        d_score(2 * v - 2 + i, i)
                for i in range(2):
                    if c:
                        c_max(2 * v + i, i)
                for i in range(2):
                    if o:
                        f_add(2 * v - 6 + i, i)
                for i in range(2):
                    if d:
                        d_pick(2 * v - 2 + i, i, is_n(v, 1))
                for i in range(2):
                    if c:
                        c_add(2 * v + i, i, is_n(v, 0))
                for i in range(2):
                    if more_c:
                        c_stats(2 * v + 2 + i, i, False)
                for i in range(2):
                    if c:
                        d_stats(2 * v + i, i)
                for i in range(2):
                    if more_c:
                        c_scale(2 * v + 2 + i, i, False)
                if f:
                    f_take(v - 2, is_n(v, 2))

            for i in range(2):
                c_stats(i, i, True)
            for i in range(2):
                c_scale(i, i, True)
            turn(0, True, False, False, False, True)
            turn(1, True, True, False, False, True)
            turn(2, True, True, True, False, True)
            with dve.Fori(3, NU - 1) as v:
                turn(v, True, True, True, True, True)
            turn(NU - 1, True, True, True, True, False)
            turn(NU, False, True, True, True, False)
            turn(NU + 1, False, False, True, True, False)
            turn(NU + 2, False, False, False, True, False)

        @block.scalar
        def _(act):
            def exponential(t, j, first):
                act.wait_ge(s["scorest_ready"], t + 1)
                if not first:
                    act.wait_ge(s["pv_done"], t - 3)
                act.activation(probs[:, j % 4, :], scoret_bank[j % 2][:, :], ACT.Exp).then_inc(s["exp_done"], 1)

            def neg_high(b, u, i):
                act.wait_ge(s["max_t"], b + 1)
                if not is_first(u):
                    act.wait_ge(neg_loaded[i], 32 * u)
                act.mul(neg_max[:, i, 0, :], t0_bank[0:NH, 0:D], -1.0).then_inc(s["neg_hi"], 1)

            def take_vt(u):
                act.wait_ge(s["ctx_t"], u + 1)
                act.copy(vt[:, bass.ds(2 * u, 2), :, :].rearrange("p b k c -> p (b k c)"),
                         t0_bank[:, :]).then_inc(s["vt_done"], 1)

            def high_k(u):
                if not is_first(u):
                    act.wait_ge(s["parts_written"], 96 * u)
                act.wait_ge(s["staged"], 32 * (u + 1))
                act.copy(k_parts[:, 0, :], ctx_stage[:, :, :].rearrange("p b n -> p (b n)")).then_inc(s["k_high"], 1)

            def mid_k(u):
                act.wait_ge(s["k_rest"], u + 1)
                act.copy(k_parts[:, 1, :], k_rest[:, :]).then_inc(s["k_mid"], 1)

            def high_q(u):
                act.wait_ge(s["q_ready"], u + 1)
                act.copy(q_parts[:, 0, :], qn[:, :, :].rearrange("p b n -> p (b n)")).then_inc(s["q_high"], 1)

            def mid_q(u):
                act.wait_ge(s["q_rest"], u + 1)
                act.copy(q_parts[:, 1, :], q_rest[:, :]).then_inc(s["q_mid"], 1)

            def take_even(b, i, first):
                act.wait_ge(s["pv_done"], NH * (b + 1))
                if not first:
                    act.wait_ge(s["div_step"], 5 * (b - 1))
                act.mul(sum_high[:, i, :], pv_bank[i][:, 0:D], high[:, 0:1])
                act.mul(num_low[:, i, :], pv_bank[i][:, 0:D], low[:, 0:1]).then_inc(s["even_taken"], 1)

            def take_xnt(b, i, first):
                act.wait_ge(s["xn_t"], b + 1)
                if not first:
                    act.wait_ge(s["yw_ready"], b - 1)
                act.copy(xnt[:, i].rearrange("p k t -> p (k t)"), t1_bank[:, 0:D]).then_inc(s["xnt_copied"], 1)

            high_k(0)
            mid_k(0)
            take_vt(0)
            high_q(0)
            mid_q(0)
            high_k(1)
            mid_k(1)
            take_vt(1)
            high_q(1)
            mid_q(1)
            neg_high(0, 0, 0)
            high_k(2)

            def unit(u, first, second, last, parts, more_parts):
                for j in range(STEPS):
                    exponential(STEPS * u + j, j, first and j < 4)
                    if j == 0:
                        neg_high(2 * u + 1, u, 1)
                    if j == 0 and parts:
                        mid_k(u + 2)
                    if j == 1 and not first:
                        take_even(2 * u - 1, 1, second)
                    if j == 2 and parts:
                        high_q(u + 2)
                    if j == 3 and not first:
                        take_xnt(2 * u - 2, 0, second)
                    if j == 4 and parts:
                        mid_q(u + 2)
                    if j == 6 and parts:
                        take_vt(u + 2)
                    if j == 9:
                        take_even(2 * u, 0, first)
                    if j == 10 and not last:
                        neg_high(2 * u + 2, u + 1, 0)
                    if j == 11 and not first:
                        take_xnt(2 * u - 1, 1, second)
                    if j == 13 and more_parts:
                        high_k(u + 3)

            unit(0, True, False, False, True, True)
            unit(1, False, True, False, True, True)
            with act.Fori(2, NU - 3) as u:
                unit(u, False, False, False, True, True)
            unit(NU - 3, False, False, False, True, False)
            unit(NU - 2, False, False, False, False, False)
            unit(NU - 1, False, False, True, False, False)
            take_even(NB - 1, 1, False)
            take_xnt(NB - 2, 0, False)
            take_xnt(NB - 1, 1, False)

            act.wait_ge(s["sh_exp"], 1)
            act.activation(logits[:, :, :], logits[:, :, :], ACT.Exp).then_inc(s["sh_exp"], 1)

            def turn(v, c, d, f):
                if c:
                    for i in range(2):
                        act.wait_ge(s["c_xn_t"], 2 * v + i + 1)
                        if not is_n(v, 0):
                            act.wait_ge(s["c_scores"], 2 * v + i - 1)
                        act.copy(xnt[:, i].rearrange("p k t -> p (k t)"), c_bank[i][:, 0:D]).then_inc(s["c_xnt"], 1)
                    for i in range(2):
                        act.wait_ge(s["c_bias"], 2 * v + i + 1)
                        if not is_n(v, 0):
                            act.wait_ge(s["c_attn_t"], 2 * v + i - 1)
                            act.wait_ge(s["c_coef"], 4 * v + 2 * i - 2)
                        act.activation(attn[:, i, :], c_bank[i][:, 256:384], ACT.Exp, bias=sc_bias[:, i:i + 1],
                                       scale=D ** -0.5, accum_out=sc_sum[:, i:i + 1]).then_inc(s["c_exp"], 1)
                    for i in range(2):
                        act.wait_ge(s["c_attn_t"], 2 * v + i + 1)
                        if not is_n(v, 0):
                            act.wait_ge(s["c_read"], 2 * v + i - 1)
                        act.copy(attn_t[:, i, :], c_bank[i][:, 384:512]).then_inc(s["c_attnt"], 1)
                if f:
                    t = v - 2
                    if not is_n(v, 2):
                        act.wait_ge(s["f_y"], t)
                    for h in range(NF):
                        act.wait_ge(s["f_h"], NF * t + (h // 4 + 1) * 4)
                        act.activation(hid[:, h, :], hid_bank[h // 4][:, (h % 4) * P:(h % 4 + 1) * P], ACT.Gelu_apprx_tanh,
                                       bias=b1s[:, h:h + 1]).then_inc(s["f_gelu"], 1)
                if d:
                    for i in range(2):
                        b = 2 * v - 2 + i
                        act.wait_ge(s["d_gath"], b + 1)
                        act.copy(zg[:, :, bass.ds(KT * b, KT)],
                                 d_bank[i][:, P:2 * P].rearrange("p (k t) -> p k t", k=2)).then_inc(s["d_zg"], 1)
                if f:
                    act.wait_ge(s["f_pt"], t + 1)
                    if not is_n(v, 2):
                        act.wait_ge(s["f_sc"], 2 * t)
                    act.copy(pick_t[:, :], pick_t_psum).then_inc(s["f_ptc"], 1)

            turn(0, True, False, False)
            turn(1, True, True, False)
            turn(2, True, True, True)
            with act.Fori(3, NU) as v:
                turn(v, True, True, True)
            turn(NU, False, True, True)
            turn(NU + 1, False, False, True)

        @block.tensor
        def _(pe):
            def scores(step, u, b_in, h, free):
                if free is not None:
                    pe.wait_ge(s["max_done"], free)
                slot = u % SLOTS
                for m in range(2):
                    ins = pe.matmul(score_bank[h % 2][:, m * D:(m + 1) * D],
                                    q_stack[0:QROWS, slot, h, b_in, m * P:(m + 1) * P],
                                    k_stack[0:QROWS, slot, h, b_in, :], start=True, stop=True)
                ins.then_inc(s["scores_ready"], 1)

            def scores_t(t, u, j, free):
                b_in, h = j // NH, j % NH
                if free:
                    pe.wait_ge(s["exp_done"], t - 1)
                if h == 0:
                    pe.wait_ge(neg_loaded[b_in], 32 * (u + 1))
                slot = u % SLOTS
                for k in range(2):
                    ins = pe.matmul(scoret_bank[j % 2][:, k * D:(k + 1) * D],
                                    k_stack[0:SROWS, slot, h, b_in, k * P:(k + 1) * P],
                                    q_stack[0:SROWS, slot, h, b_in, :], start=True, stop=True)
                ins.then_inc(s["scorest_ready"], 1)

            def values(t, b, j, first):
                i, h = j // NH, j % NH
                if h == 0:
                    pe.wait_ge(s["values_ready"], b + 1)
                    if not first:
                        pe.wait_ge(s["div_step"], 5 * (b - 2) + 2)
                pe.wait_ge(s["exp_done"], t + 1)
                pair, odd = h // 2, h % 2
                for k in range(2):
                    ins = pe.matmul(pv_bank[i][pair * Q:(pair + 1) * Q, odd * D:(odd + 1) * D],
                                    values_ones[:, i, k, pair, odd, :], probs[:, j % 4, k * D:(k + 1) * D],
                                    start=(k == 0), stop=(k == 1))
                ins.then_inc(s["pv_done"], 1)

            def max_t(b, i):
                pe.wait_ge(s["max_done"], NH * (b + 1))
                for m in range(2):
                    ins = pe.transpose(t0_bank[0:NH, m * P:(m + 1) * P], row_max[:, i, m, :], ident[:, :])
                ins.then_inc(s["max_t"], 1)

            def ctx_t(u):
                pe.wait_ge(s["staged"], 32 * (u + 1))
                for i in range(2):
                    for k in range(2):
                        ins = pe.transpose(t0_bank[:, (2 * i + k) * P:(2 * i + k + 1) * P],
                                           ctx_stage[:, i, k * P:(k + 1) * P], ident[:, :])
                ins.then_inc(s["ctx_t"], 1)

            def xn_t(b, i):
                pe.wait_ge(s["xn_ready"], b + 1)
                for k in range(2):
                    ins = pe.transpose(t1_bank[:, k * P:(k + 1) * P], xn[:, i, k * P:(k + 1) * P], ident[:, :])
                ins.then_inc(s["xn_t"], 1)

            def yw(b, i):
                pe.wait_ge(s["xnt_copied"], b + 1)
                for k in range(2):
                    ins = pe.matmul(t1_bank[:, 0:D + NE], xnt[:, i, k, :], wr_moving[:, k, :],
                                    start=(k == 0), stop=(k == 1))
                ins.then_inc(s["yw_ready"], 1)

            pe.wait_ge(s["ident_done"], 1)
            pe.wait_ge(s["ones_done"], 1)
            ctx_t(0)
            pe.wait_ge(s["vt_done"], 1)
            ctx_t(1)
            pe.wait_ge(s["stacks_loaded"], 96)
            scores(0, 0, 0, 0, None)
            scores(1, 0, 0, 1, None)
            for step in range(2, STEPS):
                scores(step, 0, step // NH, step % NH, step - 1)
                if step == NH + 1:
                    pe.wait_ge(s["vt_done"], 2)
                    max_t(0, 0)
            pe.wait_ge(s["w_ones"], 16)
            scores_t(0, 0, 0, False)
            scores_t(1, 0, 1, False)

            def unit(u, first, second, last, parts):
                for j in range(STEPS):
                    if j < STEPS - 2:
                        scores_t(STEPS * u + j + 2, u, j + 2, True)
                    elif not last:
                        scores_t(STEPS * (u + 1) + j - 14, u + 1, j - 14, True)
                    if not last:
                        if j == 0:
                            pe.wait_ge(s["stacks_loaded"], 96 * (u + 2))
                        scores(STEPS * (u + 1) + j, u + 1, j // NH, j % NH, STEPS * (u + 1) + j - 1)
                    values(STEPS * u + j, 2 * u + j // NH, j, first)
                    if j == 0:
                        pe.wait_ge(s["neg_done"], 2 * u + 1)
                        max_t(2 * u + 1, 1)
                    if j == 1 and not first:
                        if not second:
                            pe.wait_ge(s["yw_done"], 2 * u - 2)
                        xn_t(2 * u - 2, 0)
                    if j == 5 and not first:
                        if second:
                            pe.wait_ge(s["w_small"], 16 * 10)
                        yw(2 * u - 2, 0)
                    if j == 4 and parts:
                        pe.wait_ge(s["neg_done"], 2 * u + 2)
                        ctx_t(u + 2)
                    if j == 9 and not last:
                        if parts:
                            pe.wait_ge(s["vt_done"], u + 3)
                        else:
                            pe.wait_ge(s["neg_done"], 2 * u + 2)
                        max_t(2 * u + 2, 0)
                    if j == 9 and not first:
                        pe.wait_ge(s["yw_done"], 2 * u - 1)
                        xn_t(2 * u - 1, 1)
                    if j == 12 and not first:
                        yw(2 * u - 1, 1)

            unit(0, True, False, False, True)
            unit(1, False, True, False, True)
            with pe.Fori(2, NU - 2) as u:
                unit(u, False, False, False, True)
            unit(NU - 2, False, False, False, False)
            unit(NU - 1, False, False, True, False)
            for i in range(2):
                b = NB - 2 + i
                pe.wait_ge(s["yw_done"], b)
                xn_t(b, i)
                yw(b, i)

            pe.wait_ge(s["sh_exp"], 3)
            for g in range(2):
                ins = pe.transpose(t0_bank[:, g * P:(g + 1) * P],
                                   logits[:, NH * g:NH * (g + 1), :].rearrange("p b e -> p (b e)"), ident[:, :])
            ins.then_inc(s["st_t"], 1)
            with pe.Fori(0, SEARCH_BITS // BITS_A_TURN) as turn:
                for n in (turn * BITS_A_TURN + r for r in range(BITS_A_TURN)):
                    pe.wait_ge(s["counted"], n + 1)
                    pe.matmul(t1_bank[:, 0:1], same_expert[:, :], count[:, :], start=True, stop=True).then_inc(s["totalled"], 1)
            pe.wait_ge(s["counted"], SEARCH_BITS + 1)
            pe.matmul(t1_bank[:, 1:2], same_expert[:, :], count[:, :], start=True, stop=True).then_inc(s["gt_total"], 1)
            pe.wait_ge(s["eq_counted"], 1)
            pe.matmul(t1_bank[:, 2:4], earlier_batch[:, :], totals[:, :], start=True, stop=True)
            pe.matmul(t1_bank[:, 4:5], same_expert[:, :], totals[:, 0:1], start=True, stop=True).then_inc(s["eq_total"], 1)
            pe.wait_ge(s["gated_ready"], 1)
            for g in range(2):
                ins = pe.matmul(t0_bank[:, NH * g:NH * (g + 1)], gated[:, g, :], batch_of[:, :], start=True, stop=True)
            ins.then_inc(s["gate_t"], 1)

            def hidden(t, h):
                for k in range(2):
                    ins = pe.matmul(hid_bank[h // 4][:, (h % 4) * P:(h % 4 + 1) * P], w1s[:, k, h * P:(h + 1) * P],
                                    zg[:, k, bass.ds(P * t, P)], start=(k == 0), stop=(k == 1))
                ins.then_inc(s["f_h"], 1)

            def turn(v, c, d, f, o):
                t = v - 2
                if c:
                    for i in range(2):
                        b = 2 * v + i
                        pe.wait_ge(s["c_xn"], b + 1)
                        if not is_n(v, 0):
                            pe.wait_ge(s["c_x3"], b - 1)
                        for k in range(2):
                            ins = pe.transpose(c_bank[i][:, k * P:(k + 1) * P], xn[:, i, k * P:(k + 1) * P], ident[:, :])
                        ins.then_inc(s["c_xn_t"], 1)
                if f:
                    if is_n(v, 2):
                        pe.wait_ge(s["w_big"], 16 * 3)
                    pe.wait_ge(s["d_zg"], 2 * t + 2)
                    if not is_n(v, 2):
                        pe.wait_ge(s["f_gelu"], NF * t)
                    for h in range(0, 4):
                        hidden(t, h)
                if c:
                    for i in range(2):
                        b = 2 * v + i
                        pe.wait_ge(s["c_xnt"], b + 1)
                        for k in range(2):
                            pe.matmul(c_bank[i][:, 256:384], xnt[:, i, k, :], vt[:, b, k, :],
                                      start=(k == 0), stop=False)
                        ins = pe.matmul(c_bank[i][:, 256:384], ones_bf[0:1, 0:P], mask_bias[:, b, :], start=False, stop=True)
                        ins.then_inc(s["c_scores"], 1)
                if o:
                    pe.wait_ge(s["f_taken"], t)
                    pe.wait_ge(s["f_ptc"], t)
                    for i in range(2):
                        pe.matmul(put_bank[i][:, 0:D], pick_t[i * KT:(i + 1) * KT, :],
                                  taken_out[i * KT:(i + 1) * KT, :], start=True, stop=True).then_inc(s["f_sc"], 1)
                if d:
                    for i in range(2):
                        b = 2 * v - 2 + i
                        pe.wait_ge(s["d_score"], b + 1)
                        if not is_n(v, 1):
                            pe.wait_ge(s["d_zg"], b - 1)
                        pe.transpose(d_bank[i][:, 0:P], score[:, i:i + 1].to_broadcast([P, P]), ident[:, :]).then_inc(s["d_row"], 1)
                if f:
                    for h in range(4, 6):
                        hidden(t, h)
                if c:
                    for i in range(2):
                        pe.wait_ge(s["c_exp"], 2 * v + i + 1)
                        pe.transpose(c_bank[i][:, 384:512], attn[:, i, :], ident[:, :]).then_inc(s["c_attn_t"], 1)
                if f:
                    for h in range(6, 8):
                        hidden(t, h)
                if c:
                    for i in range(2):
                        b = 2 * v + i
                        pe.wait_ge(s["c_attnt"], b + 1)
                        pe.matmul(c_bank[i][:, 0:D], attn_t[:, i, :], ctx[:, b, :], start=True, stop=True).then_inc(s["c_read"], 1)
                if d:
                    for i in range(2):
                        b = 2 * v - 2 + i
                        pe.wait_ge(s["d_pick"], b + 1)
                        for k in range(2):
                            ins = pe.matmul(d_bank[i][:, P + k * KT:P + (k + 1) * KT], z[:, i, k * P:(k + 1) * P],
                                            pick[:, i, :], start=True, stop=True)
                        ins.then_inc(s["d_gath"], 1)
                if f:
                    pe.wait_ge(s["d_pickbf"], 2 * t + 2)
                    if not is_n(v, 2):
                        pe.wait_ge(s["f_out"], 2 * t)
                    pe.transpose(pick_t_psum, pick_bf[:, bass.ds(2 * t, 2), :].rearrange("p b k -> p (b k)"),
                                 ident_bf[:, :]).then_inc(s["f_pt"], 1)
                    if not is_n(v, 2):
                        pe.wait_ge(s["f_taken"], t)
                    for h in range(NF):
                        pe.wait_ge(s["f_gelu"], NF * t + h + 1)
                        ins = pe.matmul(y_bank[:, 0:D], hid[:, h, :], w2s[:, h, :], start=(h == 0), stop=(h == NF - 1))
                    ins.then_inc(s["f_y"], 1)

            turn(0, True, False, False, False)
            turn(1, True, True, False, False)
            turn(2, True, True, True, False)
            with pe.Fori(3, NU) as v:
                turn(v, True, True, True, True)
            turn(NU, False, True, True, True)
            turn(NU + 1, False, False, True, True)
            turn(NU + 2, False, False, False, True)



_INS = ['x', 'ctx_2048', 'mask_BxS2_bk0', 'L0_ffn_router_w', 'L0_ffn_router_b', 'L0_ffn_expert_w',
        'L0_ffn_expert_b', 'L1_ffn_w_r', 'L1_ffn_b_r', 'L1_ffn_w1', 'L1_ffn_b1', 'L1_ffn_w2', 'L1_ffn_b2']
_OUTS = [((16, 128, 256), 'float32')]


def kernel(**inputs):
    import numpy as _np
    import concourse.bacc as _bacc
    from concourse import mybir as _mybir
    from concourse.bass_utils import run_bass_kernel_spmd as _run

    nc = _bacc.Bacc("TRN2", target_bir_lowering=False, num_devices=1)
    arrays, args = {}, []
    for name in _INS:
        a = _np.ascontiguousarray(inputs[name])
        if a.ndim == 0:
            a = a.reshape(1)
        arrays[f"in_{name}_dram"] = a
        args.append(nc.dram_tensor(f"in_{name}_dram", a.shape, _mybir.dt.from_np(a.dtype), kind="ExternalInput").ap())
    for i, (shape, dtype) in enumerate(_OUTS):
        dt = _mybir.dt.from_np(_np.dtype(dtype))
        args.append(nc.dram_tensor(f"out_{i}_dram", shape, dt, kind="ExternalOutput").ap())
    build_program(nc, *args)
    r = _run(nc, [arrays], core_ids=[0])
    return r.results[0]["out_0_dram"]
```

```python
from contextlib import ExitStack

import concourse.bass as bass
from concourse import mybir

F32 = mybir.dt.float32
BF16 = mybir.dt.bfloat16
I32 = mybir.dt.int32
U8 = mybir.dt.uint8
ALU = mybir.AluOpType
ACT = mybir.ActivationFunctionType
AX = mybir.AxisListType

P = 128
NB = 16
D = 256
NH = 8
C = P // NH
Q = 32
NU = NB // 2
STEPS = 2 * NH
NE = 16
KE = NB * P // NE
KT = P // 2
DF = 4 * D
NF = DF // P
EPS = 1e-5
MASKED = -1e30
SLOTS = 3
QROWS = 6 * C
SROWS = QROWS + 2
DIGITS = 15
HIGH_DIGITS = 7
DIGITS_A_TURN = 4


def build_program(nc, x, ctx_2048, mask, router_w, router_b, expert_w, expert_b,
                  w_r, b_r, w1, b1, w2, b2, out):
    with ExitStack() as stack:
        def sb(name, shape, dt=F32):
            return stack.enter_context(nc.sbuf_tensor(name, shape, dt))

        def bank(name):
            return stack.enter_context(nc.psum_tensor(name, [P, 512], F32))

        def sem(name):
            return stack.enter_context(nc.semaphore(name))

        q_parts_dram = nc.dram_tensor("q_parts_dram", (NU, 3, C, NH, 2 * D), BF16, kind="Internal").ap()
        k_parts_dram = nc.dram_tensor("k_parts_dram", (NU, 3, C, NH, 2 * D), BF16, kind="Internal").ap()

        xs = sb("xs", [P, NB, D])
        ctx = sb("ctx", [P, NB, D])
        ctx_stage = sb("ctx_stage", [P, 2, D])
        x_stage = sb("x_stage", [P, 2, D])
        x_new = sb("x_new", [P, 2, D])
        x_new3 = sb("x_new3", [P, 2, D])
        vt = sb("vt", [P, NB, 2, P])
        values_ones = sb("values_ones", [P, 2, 2, NH // 2, 2, Q])
        y = sb("y", [P, NB, D])
        q_stack = sb("q_stack", [P, SLOTS, NH, 2, D], BF16)
        k_stack = sb("k_stack", [P, SLOTS, NH, 2, D], BF16)
        probs = sb("probs", [P, 4, 512])
        mv0 = sb("mv0", [P, 2, 2])
        st = sb("st", [P, 2, 6])
        var16 = sb("var16", [P, 2])
        rstd_q = sb("rstd_q", [P, 2])
        minus_half = sb("minus_half", [P, 2])
        qn = sb("qn", [P, 2, D])
        q_rest = sb("q_rest", [P, 2 * D])
        q_parts = sb("q_parts", [P, 3, 2 * D], BF16)
        k_rest = sb("k_rest", [P, 2 * D])
        k_parts = sb("k_parts", [P, 3, 2 * D], BF16)
        row_max = sb("row_max", [P, 2, 2, NH])
        neg_max = sb("neg_max", [NH, 2, 2, D], BF16)
        low = sb("low", [P, 1])
        high = sb("high", [P, 1])
        num_low = sb("num_low", [P, 2, D])
        sum_high = sb("sum_high", [P, 2, D])
        numer = sb("numer", [P, 2, D])
        denom = sb("denom", [P, 2, D])
        denom_inv = sb("denom_inv", [P, 2, D])
        denom_own = sb("denom_own", [P, 2, D])
        mv = sb("mv", [P, 2, 2])
        var_eps = sb("var_eps", [P, 2])
        rstd = sb("rstd", [P, 2])
        xn = sb("xn", [P, 2, D])
        xnt = sb("xnt", [P, 2, 2, P])
        wr_moving = sb("wr_moving", [P, 2, D + NE])
        eb_rows = sb("eb_rows", [P, D + NE])
        logits = sb("logits", [P, NB, NE])
        lg_max = sb("lg_max", [P, NB])
        lg_sum = sb("lg_sum", [P, NB])
        lg_inv = sb("lg_inv", [P, NB])
        st_probs = sb("st_probs", [P, 2, P])
        st_high = sb("st_high", [P, 2, P], BF16)
        ident = sb("ident", [P, P])
        ident_bf = sb("ident_bf", [P, P], BF16)
        earlier = sb("earlier", [P, P])
        same_expert = sb("same_expert", [P, P], BF16)
        earlier_batch = sb("earlier_batch", [P, P], BF16)
        batch_of = sb("batch_of", [P, NH])
        free_i = sb("free_i", [P, P], I32)
        part_i = sb("part_i", [P, 1], I32)
        work_i = sb("work_i", [P, P], I32)
        work_p = sb("work_p", [P, 2], I32)
        half_i = sb("half_i", [P, 1], I32)
        free_f = sb("free_f", [P, P])
        part_f = sb("part_f", [P, 1])
        free_lo = sb("free_lo", [P, P])
        free_hi = sb("free_hi", [P, P])
        part_lo = sb("part_lo", [P, 1])
        part_hi = sb("part_hi", [P, 1])
        ones = sb("ones", [P, P])
        ones_bf = sb("ones_bf", [2, 2 * D], BF16)
        junk = sb("junk", [P, 2, P])
        trial = sb("trial", [P, 2, 3], I32)
        thr = sb("thr", [P, 1], I32)
        cand = sb("cand", [P, 3], I32)
        taken = sb("taken", [P, 1], I32)
        count = sb("count", [P, 3], BF16)
        reached = sb("reached", [P, 3])
        digit = sb("digit", [P, 1])
        above = sb("above", [P, 2, P])
        equal = sb("equal", [P, 2, P])
        high_marks = [m[:, 0, :].bitcast(BF16).rearrange("p (g t) -> p g t", g=2) for m in (junk, above, equal)]
        running = sb("running", [P, 2, P])
        totals = sb("totals", [P, 2], BF16)
        base = sb("base", [P, 2])
        need = sb("need", [P, 1])
        gated = sb("gated", [P, 2, P])
        gate = sb("gate", [P, NB])
        mask_u8 = sb("mask_u8", [P, NB, P], U8)
        mask_bias = sb("mask_bias", [1, NB, P], BF16)
        valid = sb("valid", [P, NB])
        sc_max = sb("sc_max", [P, 2])
        sc_bias = sb("sc_bias", [P, 2])
        sc_sum = sb("sc_sum", [P, 2])
        sc_inv = sb("sc_inv", [P, 2])
        sc_coef = sb("sc_coef", [P, 2])
        attn = sb("attn", [P, 2, P])
        attn_t = sb("attn_t", [P, 2, P])
        st3 = sb("st3", [P, 2, 6])
        mv3 = sb("mv3", [P, 2, 2])
        var_eps3 = sb("var_eps3", [P, 2])
        rstd3 = sb("rstd3", [P, 2])
        z = sb("z", [P, 2, D])
        z_work = sb("z_work", [P, 2, D])
        wr_rows = sb("wr_rows", [P, D])
        br_rows = sb("br_rows", [P, 1])
        score0 = sb("score0", [P, 2])
        score = sb("score", [P, 2])
        rank_gt = sb("rank_gt", [P, 2])
        rank_eq = sb("rank_eq", [P, 2])
        rank = sb("rank", [P, 2])
        cmp_work = sb("cmp_work", [P, 2, P])
        pick = sb("pick", [P, 2, KT])
        pick_bf = sb("pick_bf", [P, NB, KT], BF16)
        zg = q_stack[:, 0].rearrange("p h b n -> p (h b n)").bitcast(F32).rearrange("p (k t) -> p k t", k=2)
        w1s = k_stack[:, 0].rearrange("p h b n -> p (h b n)").bitcast(F32).rearrange("p (k f) -> p k f", k=2)
        w2s = k_stack[:, 1].rearrange("p h b n -> p (h b n)").bitcast(F32).rearrange("p (k n) -> p k n", k=NF)
        b1s = sb("b1s", [P, NF])
        b2_rows = sb("b2_rows", [P, D])
        hid = probs[:, 0:2, :].rearrange("p s (f t) -> p (s f) t", f=4)
        taken_out = sb("taken_out", [P, D])
        pick_t = sb("pick_t", [P, P])
        out_rows = y

        score_bank = [bank("score_bank0"), bank("score_bank1")]
        scoret_bank = [bank("scoret_bank0"), bank("scoret_bank1")]
        pv_bank = [bank("pv_bank0"), bank("pv_bank1")]
        first_score_bank = score_bank + pv_bank
        t0_bank = bank("t0_bank")
        t1_bank = bank("t1_bank")

        c_bank, d_bank = score_bank, scoret_bank
        hid_bank, y_bank, put_bank = pv_bank, t0_bank, [t1_bank, t0_bank]
        pick_t_psum = t1_bank[:, 0:P // 2].bitcast(BF16)

        names = """passed kept w_ones x_loaded ctx_loaded staged parts_written stacks_loaded w_small w_big mask_loaded
        iota_done ident_done consts_done ones_done k_high k_rest k_mid k_split q_ready q_high q_rest q_mid q_split stats_q var_q root_q
        var1 root1 values_ready even_taken div_step bn1
        scores_ready max_done scorest_ready exp_done pv_done max_t ctx_t vt_done neg_hi neg_done
        x1_done stats1 xn_ready xn_t xnt_copied yw_ready yw_done
        bn_q sh_exp st_t cand_ready counted totalled gt_total eq_counted eq_total gated_ready gate_t
        c_bn c_stats c_var c_root c_xn c_xn_t c_xnt c_scores c_max c_bias c_exp c_attn_t c_attnt c_coef c_read c_x3
        d_bn d_stats d_var d_root d_z d_dot d_score d_rank d_row d_pick d_pickbf d_gath d_zg
        f_h f_gelu f_y f_taken f_pt f_ptc f_sc f_out out_stored""".split()
        s = {n: sem("s_" + n) for n in names}
        neg_loaded = [sem("s_neg_loaded0"), sem("s_neg_loaded1")]

        block = stack.enter_context(nc.Block())

        def is_first(u):
            return isinstance(u, int) and u == 0

        def is_n(u, n):
            return isinstance(u, int) and u == n

        def wait_apart(eng, semaphore, value):
            eng.wait_ge(semaphore, value)
            eng.sem_inc(s["passed"], 1)

        @block.sync
        def _(sp):
            x_rows = x.rearrange("b c n -> c b n")
            ctx_rows = ctx_2048.rearrange("b c n -> c b n")

            def load_stage(u):
                if not is_first(u):
                    sp.wait_ge(s["ctx_t"], u)
                    sp.wait_ge(s["k_split"], u)
                    sp.wait_ge(s["q_split"], u)
                sp.dma_start(ctx_stage[:, :, :], ctx_rows[:, bass.ds(2 * u, 2), :]).then_inc(s["staged"], 16)
                sp.dma_start(x_stage[:, :, :], x_rows[:, bass.ds(2 * u, 2), :]).then_inc(s["staged"], 16)

            def load_x(u):
                sp.dma_start(xs[:, bass.ds(2 * u, 2), :], x_rows[:, bass.ds(2 * u, 2), :]).then_inc(s["x_loaded"], 16)

            def write_k_parts(u):
                sp.wait_ge(s["k_split"], u + 1)
                for part in range(3):
                    sp.dma_start(k_parts_dram[u, part].rearrange("d h n -> h d n"),
                                 k_parts[:, part, :]).then_inc(s["parts_written"], 16)

            def write_q_parts(u):
                sp.wait_ge(s["q_split"], u + 1)
                for part in range(3):
                    sp.dma_start(q_parts_dram[u, part].rearrange("d h n -> h d n"),
                                 q_parts[:, part, :]).then_inc(s["parts_written"], 16)

            def load_stacks(u, reused):
                slot = u % SLOTS
                wait_apart(sp, s["parts_written"], 96 * (u + 1))
                if not is_first(u):
                    wait_apart(sp, s["stacks_loaded"], 96 * u)
                if reused:
                    wait_apart(sp, s["scorest_ready"], STEPS * (u - SLOTS + 1))
                k_rows = k_parts_dram[u].rearrange("p d h n -> (p d) (h n)")
                q_rows = q_parts_dram[u].rearrange("p d h n -> p d (h n)")
                k_to = k_stack[:, slot].rearrange("p h b n -> p (h b n)")
                q_to = q_stack[:, slot].rearrange("p h b n -> p (h b n)")
                n = NH * 2 * D
                sp.dma_start(k_to[0:3 * C], k_rows).then_inc(s["stacks_loaded"], 16)
                sp.dma_start(k_to[3 * C:5 * C], k_rows[0:2 * C]).then_inc(s["stacks_loaded"], 16)
                sp.dma_start(k_to[5 * C:6 * C], k_rows[0:C]).then_inc(s["stacks_loaded"], 16)
                sp.dma_start(q_to[0:3 * C], q_rows[0:1].to_broadcast([3, C, n])).then_inc(s["stacks_loaded"], 16)
                sp.dma_start(q_to[3 * C:5 * C], q_rows[1:2].to_broadcast([2, C, n])).then_inc(s["stacks_loaded"], 16)
                sp.dma_start(q_to[5 * C:6 * C], q_rows[2]).then_inc(s["stacks_loaded"], 16)

            def load_neg_max(u, i):
                wait_apart(sp, s["neg_done"], 2 * u + i + 1)
                for part in range(2):
                    sp.dma_start(q_stack[QROWS + part:QROWS + part + 1, u % SLOTS, :, i, :],
                                 neg_max[:, i, part, :]).then_inc(neg_loaded[i], 16)

            def load_small():
                for half in range(2):
                    sp.dma_start(wr_moving[:, half, 0:D], expert_w[half * P:(half + 1) * P, :]).then_inc(s["w_small"], 16)
                    sp.dma_start(wr_moving[:, half, D:D + NE], router_w[half * P:(half + 1) * P, :]).then_inc(s["w_small"], 16)
                for dst, row in ((eb_rows[:, 0:D], expert_b), (eb_rows[:, D:D + NE], router_b),
                                 (wr_rows[:, :], w_r), (b2_rows[:, :], b2)):
                    sp.dma_start(dst, row.rearrange("(a n) -> a n", a=1).to_broadcast([P, row.shape[0]])).then_inc(s["w_small"], 16)
                sp.dma_start(br_rows[:, :], b_r.to_broadcast([P, 1])).then_inc(s["w_small"], 16)
                with nc.allow_non_contiguous_dma(reason="1024 single biases, one per partition and block"):
                    sp.dma_start(b1s[:, :], b1.rearrange("(k p) -> p k", p=P)).then_inc(s["w_big"], 16)

            load_stage(0)
            sp.dma_start(mask_u8[:, :, :], mask.rearrange("(a b) m -> a b m", a=1).to_broadcast([P, NB, P])).then_inc(s["mask_loaded"], 16)
            sp.wait_ge(s["ones_done"], 1)
            sp.dma_start(k_stack[QROWS:SROWS].rearrange("p s h b n -> p (s h) (b n)"),
                         ones_bf[:, :].unsqueeze(1).to_broadcast([2, SLOTS * NH, 2 * D])).then_inc(s["w_ones"], 16)
            write_k_parts(0)
            write_q_parts(0)
            load_stage(1)
            load_stacks(0, False)
            write_k_parts(1)
            write_q_parts(1)
            load_stage(2)
            load_stacks(1, False)
            sp.wait_ge(neg_loaded[0], 32)
            load_x(0)
            load_small()

            def unit(u, more_stage, more_parts, more_x, reused):
                load_neg_max(u, 1)
                if more_x:
                    wait_apart(sp, s["x_loaded"], 16 * (u + 1))
                    load_x(u + 1)
                if more_parts:
                    write_k_parts(u + 2)
                    write_q_parts(u + 2)
                    if more_stage:
                        load_stage(u + 3)
                    load_stacks(u + 2, reused)
                if more_x:
                    load_neg_max(u + 1, 0)

            unit(0, True, True, True, False)
            unit(1, True, True, True, True)
            with sp.Fori(2, NU - 3) as u:
                unit(u, True, True, True, True)
            unit(NU - 3, False, True, True, True)
            unit(NU - 2, False, False, True, True)
            unit(NU - 1, False, False, False, True)
            sp.wait_ge(s["scorest_ready"], STEPS * NU)
            sp.dma_start(ctx[:, :, :], ctx_rows).then_inc(s["ctx_loaded"], 16)
            sp.dma_start(w1s, w1.rearrange("(k p) f -> p k f", p=P)).then_inc(s["w_big"], 16)
            sp.dma_start(w2s, w2.rearrange("(k p) f -> p k f", p=P)).then_inc(s["w_big"], 16)

            def store(t):
                sp.wait_ge(s["f_out"], 2 * t + 2)
                sp.dma_start(out.rearrange("b t n -> t b n")[:, bass.ds(2 * t, 2), :],
                             out_rows[:, bass.ds(2 * t, 2), :]).then_inc(s["out_stored"], 16)

            with sp.Fori(0, NU) as t:
                store(t)
            sp.wait_ge(s["out_stored"], 16 * NU)

        @block.gpsimd
        def _(pool):
            pool.iota(free_i[:, :], pattern=[[1, P]], base=0, channel_multiplier=0).then_inc(s["iota_done"], 1)
            pool.wait_ge(s["iota_done"], 1)
            pool.iota(part_i[:, :], pattern=[[0, 1]], base=0, channel_multiplier=1).then_inc(s["iota_done"], 1)
            pool.wait_ge(s["ones_done"], 1)

            def rest_k(u):
                wait_apart(pool, s["k_high"], u + 1)
                pool.tensor_tensor(k_rest[:, :], ctx_stage[:, :, :].rearrange("p b n -> p (b n)"), k_parts[:, 0, :],
                                   ALU.subtract).then_inc(s["k_rest"], 1)

            def low_k(u):
                wait_apart(pool, s["k_mid"], u + 1)
                pool.tensor_tensor(k_parts[:, 2, :], k_rest[:, :], k_parts[:, 1, :], ALU.subtract).then_inc(s["k_split"], 1)

            def rest_q(u):
                wait_apart(pool, s["q_high"], u + 1)
                pool.tensor_tensor(q_rest[:, :], qn[:, :, :].rearrange("p b n -> p (b n)"), q_parts[:, 0, :],
                                   ALU.subtract).then_inc(s["q_rest"], 1)

            def low_q(u):
                wait_apart(pool, s["q_mid"], u + 1)
                pool.tensor_tensor(q_parts[:, 2, :], q_rest[:, :], q_parts[:, 1, :], ALU.subtract).then_inc(s["q_split"], 1)

            def inverse_root(dst, variance, work, factor, known, summed, ready, n):
                wait_apart(pool, s[known], n + 1)
                pool.tensor_scalar(work, variance, EPS, factor, ALU.add, ALU.mult).then_inc(s[summed], 1)
                wait_apart(pool, s[summed], n + 1)
                pool.tensor_tensor(dst, work, minus_half[:, 0:dst.shape[1]], ALU.pow).then_inc(s[ready], 1)

            def root_q(u):
                inverse_root(rstd_q[:, :], mv0[:, :, 1], var16[:, :], float(C), "stats_q", "var_q", "root_q", u)

            def root_rows(b, i):
                inverse_root(rstd[:, i:i + 1], mv[:, i, 1:2], var_eps[:, i:i + 1], 1.0, "stats1", "var1", "root1", b)

            def keep_rows(rows, b, i):
                pool.tensor_copy(xs[:, b, :], rows[:, i, :]).then_inc(s["kept"], 1)

            def fill_values(b, u, i, first):
                if not first:
                    pool.wait_ge(s["pv_done"], NH * (b - 1))
                wait_apart(pool, s["vt_done"], u + 1)
                for odd in range(2):
                    from_ = vt[:, b, :, :].rearrange("p k (q o c) -> p k q o c", q=NH // 2, o=2)[:, :, :, odd, :]
                    ins = pool.tensor_copy(values_ones[:, i, :, :, odd, odd * C:odd * C + C], from_)
                ins.then_inc(s["values_ready"], 1)

            root_q(0)
            root_q(1)
            fill_values(0, 0, 0, True)
            rest_k(2)
            root_q(2)

            def unit(u, first, parts, more_parts, last):
                if parts:
                    low_k(u + 2)
                    rest_q(u + 2)
                fill_values(2 * u + 1, u, 1, first)
                if parts:
                    low_q(u + 2)
                if not first:
                    root_rows(2 * u - 1, 1)
                    keep_rows(x_new, 2 * u - 1, 1)
                if not last:
                    fill_values(2 * u + 2, u + 1, 0, False)
                root_rows(2 * u, 0)
                keep_rows(x_new, 2 * u, 0)
                if more_parts:
                    rest_k(u + 3)
                    root_q(u + 3)

            unit(0, True, True, True, False)
            with pool.Fori(1, NU - 3) as u:
                unit(u, False, True, True, False)
            unit(NU - 3, False, True, False, False)
            unit(NU - 2, False, False, False, False)
            unit(NU - 1, False, False, False, True)
            root_rows(NB - 1, 1)
            keep_rows(x_new, NB - 1, 1)

            def c_roots(t):
                for i in range(2):
                    inverse_root(rstd[:, i:i + 1], mv[:, i, 1:2], var_eps[:, i:i + 1], 1.0,
                                 "c_stats", "c_var", "c_root", 2 * t + i)

            def turn(v, c, d, more_c):
                if d:
                    for i in range(2):
                        b = 2 * v - 2 + i
                        wait_apart(pool, s["d_pick"], b + 1)
                        pool.tensor_copy(pick_bf[:, b, :], pick[:, i, :]).then_inc(s["d_pickbf"], 1)
                if more_c:
                    c_roots(v + 1)
                if c:
                    for i in range(2):
                        inverse_root(rstd3[:, i:i + 1], mv3[:, i, 1:2], var_eps3[:, i:i + 1], 1.0,
                                     "d_stats", "d_var", "d_root", 2 * v + i)
                    for i in range(2):
                        keep_rows(x_new3, 2 * v + i, i)

            c_roots(0)
            turn(0, True, False, True)
            with pool.Fori(1, NU - 1) as v:
                turn(v, True, True, True)
            turn(NU - 1, True, True, False)
            turn(NU, False, True, False)

        @block.vector
        def _(dve):
            dve.memset(minus_half[:, :], -0.5)
            dve.memset(values_ones[:, :, :, :, :, :], 1.0)
            dve.memset(ones[:, :], 1.0)
            dve.memset(ones_bf[:, :], 1.0).then_inc(s["ones_done"], 1)
            dve.wait_ge(s["iota_done"], 2)
            k = [0]

            def link(ins):
                k[0] += 1
                ins.then_inc(s["consts_done"], 1)
                dve.wait_ge(s["consts_done"], k[0])

            dve.tensor_copy(free_f[:, :], free_i[:, :])
            link(dve.tensor_copy(part_f[:, :], part_i[:, :]))
            dve.tensor_scalar(ident[:, :], free_f[:, :], part_f[:, 0:1], None, ALU.is_equal).then_inc(s["ident_done"], 1)
            dve.wait_ge(s["ident_done"], 1)

            def stats_q(u):
                if not is_first(u):
                    dve.wait_ge(s["q_split"], u)
                dve.wait_ge(s["staged"], 32 * (u + 1))
                for i in range(2):
                    dve.bn_stats(st[:, i, :], x_stage[:, i, :]).then_inc(s["bn_q"], 1)
                wait_apart(dve, s["bn_q"], 2 * u + 2)
                dve.bn_aggr(mv0[:, 0, :], st[:, 0, :])
                dve.bn_aggr(mv0[:, 1, :], st[:, 1, :]).then_inc(s["stats_q"], 1)

            def scale_q(u):
                dve.wait_ge(s["root_q"], u + 1)
                for i in range(2):
                    ins = dve.tensor_scalar(qn[:, i, :], x_stage[:, i, :], mv0[:, i, 0:1], rstd_q[:, i:i + 1],
                                            ALU.subtract, ALU.mult)
                ins.then_inc(s["q_ready"], 1)

            def split_first(u):
                high, middle = k_parts[:, 0, :], k_parts[:, 1, :]
                dve.wait_ge(s["k_high"], u + 1)
                dve.tensor_tensor(k_rest[:, :], ctx_stage[:, :, :].rearrange("p b n -> p (b n)"), high,
                                  ALU.subtract).then_inc(s["k_rest"], 1)
                scale_q(u)
                dve.wait_ge(s["k_mid"], u + 1)
                dve.tensor_tensor(k_parts[:, 2, :], k_rest[:, :], middle, ALU.subtract).then_inc(s["k_split"], 1)
                high, middle = q_parts[:, 0, :], q_parts[:, 1, :]
                dve.wait_ge(s["q_high"], u + 1)
                dve.tensor_tensor(q_rest[:, :], qn[:, :, :].rearrange("p b n -> p (b n)"), high,
                                  ALU.subtract).then_inc(s["q_rest"], 1)
                dve.wait_ge(s["q_mid"], u + 1)
                dve.tensor_tensor(q_parts[:, 2, :], q_rest[:, :], middle, ALU.subtract).then_inc(s["q_split"], 1)

            stats_q(0)
            split_first(0)
            link(dve.tensor_scalar(earlier[:, :], free_f[:, :], part_f[:, 0:1], None, ALU.is_lt))
            dve.tensor_copy(ident_bf[:, :], ident[:, :])
            link(dve.tensor_scalar(work_i[:, :], free_i[:, :], 15, None, ALU.bitwise_and))
            link(dve.tensor_scalar(work_p[:, 0:1], part_i[:, :], 15, None, ALU.bitwise_and))
            link(dve.tensor_scalar(work_p[:, 1:2], part_i[:, :], 4, None, ALU.logical_shift_right))
            dve.tensor_copy(free_lo[:, :], work_i[:, :])
            dve.tensor_copy(part_lo[:, :], work_p[:, 0:1])
            link(dve.tensor_scalar(half_i[:, :], work_p[:, 1:2], 1, None, ALU.bitwise_and))
            link(dve.tensor_copy(high[:, :], half_i[:, :]))
            dve.tensor_scalar(low[:, :], high[:, :], -1.0, 1.0, ALU.mult, ALU.add)
            link(dve.tensor_copy(part_hi[:, :], work_p[:, 1:2]))
            link(dve.tensor_scalar(work_i[:, :], free_i[:, :], 4, None, ALU.logical_shift_right))
            link(dve.tensor_copy(free_hi[:, :], work_i[:, :]))
            dve.tensor_scalar(batch_of[:, :], free_f[:, 0:NH], part_hi[:, 0:1], None, ALU.is_equal)
            link(dve.tensor_scalar(same_expert[:, :], free_lo[:, :], part_lo[:, 0:1], None, ALU.is_equal))
            link(dve.scalar_tensor_tensor(earlier_batch[:, :], free_hi[:, :], part_hi[:, 0:1], same_expert[:, :],
                                          ALU.is_gt, ALU.mult))
            n_consts = k[0]

            def maximum(step, b, h, i, first_h):
                if first_h:
                    dve.wait_ge(s["max_t"], b - 1)
                dve.wait_ge(s["scores_ready"], step + 1)
                dve.tensor_reduce(row_max[:, i, :, h], score_bank[h % 2][:, :].rearrange("p (m n) -> p m n", m=2),
                                  AX.X, ALU.max).then_inc(s["max_done"], 1)

            def neg_low(b, i):
                dve.wait_ge(s["neg_hi"], b + 1)
                dve.scalar_tensor_tensor(neg_max[:, i, 1, :], t0_bank[0:NH, 0:D], -1.0, neg_max[:, i, 0, :],
                                         ALU.mult, ALU.subtract).then_inc(s["neg_done"], 1)

            def gather_parts(b, i):
                odd_heads = pv_bank[i][:, D:2 * D]
                dve.wait_ge(s["even_taken"], b + 1)
                dve.scalar_tensor_tensor(denom[:, i, :], odd_heads, low[:, 0:1], sum_high[:, i, :],
                                         ALU.mult, ALU.add).then_inc(s["div_step"], 1)
                dve.scalar_tensor_tensor(numer[:, i, :], odd_heads, high[:, 0:1], num_low[:, i, :],
                                         ALU.mult, ALU.add).then_inc(s["div_step"], 1)

            def invert(b, i):
                dve.wait_ge(s["div_step"], 5 * b + 1)
                dve.reciprocal(denom_inv[:, i, :], denom[:, i, :]).then_inc(s["div_step"], 1)

            def bring_over(b, i):
                wait_apart(dve, s["div_step"], 5 * b + 3)
                dve.stream_shuffle(out=denom_own[:, i, :], in_=denom_inv[:, i, :],
                                   mask=[(n + C) % Q for n in range(Q)]).then_inc(s["div_step"], 1)
                dve.wait_ge(s["div_step"], 5 * b + 4)
                dve.tensor_tensor(numer[:, i, :], numer[:, i, :], denom_own[:, i, :], ALU.mult).then_inc(s["div_step"], 1)

            def add_x1(b, u, i, first):
                dve.wait_ge(s["div_step"], 5 * b + 5)
                dve.wait_ge(s["x_loaded"], 16 * (u + 1))
                if not first:
                    dve.wait_ge(s["kept"], b - 1)
                dve.tensor_tensor(x_new[:, i, :], numer[:, i, :], xs[:, b, :], ALU.add).then_inc(s["x1_done"], 1)
                dve.wait_ge(s["x1_done"], b + 1)
                dve.bn_stats(st3[:, i, :], x_new[:, i, :]).then_inc(s["bn1"], 1)
                wait_apart(dve, s["bn1"], b + 1)
                dve.bn_aggr(mv[:, i, :], st3[:, i, :]).then_inc(s["stats1"], 1)

            def scale_rows(b, i, first):
                if not first:
                    dve.wait_ge(s["xn_t"], b - 1)
                dve.wait_ge(s["root1"], b + 1)
                dve.tensor_scalar(xn[:, i, :], x_new[:, i, :], mv[:, i, 0:1], rstd[:, i:i + 1],
                                  ALU.subtract, ALU.mult).then_inc(s["xn_ready"], 1)

            def take_yw(b):
                dve.wait_ge(s["yw_ready"], b + 1)
                if is_n(b, 0):
                    dve.wait_ge(s["w_small"], 16 * 9)
                dve.tensor_tensor(y[:, b, :], t1_bank[:, 0:D], eb_rows[:, 0:D], ALU.add)
                dve.tensor_tensor(logits[:, b, :], t1_bank[:, D:D + NE], eb_rows[:, D:D + NE], ALU.add).then_inc(s["yw_done"], 1)

            def unit(u, first, second, last, parts, more_parts):
                a, b = 2 * u - 1, 2 * u
                for j in range(STEPS):
                    if not last:
                        maximum(STEPS * (u + 1) + j, 2 * (u + 1) + j // NH, j % NH, j // NH, j % NH == 0)
                    if j == 1:
                        neg_low(2 * u + 1, 1)
                    if j == 1 and not first:
                        gather_parts(a, 1)
                    if j == 1 and parts:
                        scale_q(u + 2)
                    if j == 2 and not first:
                        invert(a, 1)
                    if j == 3 and not first:
                        bring_over(a, 1)
                    if j == 4 and not first:
                        add_x1(a, u - 1, 1, second)
                    if j == 7 and not first:
                        take_yw(2 * u - 2)
                    if j == 6 and not first:
                        scale_rows(a, 1, second)
                    if j == 9 and not last:
                        neg_low(2 * u + 2, 0)
                    if j == 9:
                        gather_parts(b, 0)
                    if j == 10:
                        invert(b, 0)
                    if j == 11:
                        bring_over(b, 0)
                    if j == 12:
                        add_x1(b, u, 0, first)
                    if j == 13 and not first:
                        take_yw(a)
                    if j == 14:
                        scale_rows(b, 0, first)
                    if j == 15 and more_parts:
                        stats_q(u + 3)

            dve.wait_ge(s["mask_loaded"], 16)
            dve.tensor_scalar(mask_bias[:, :, :], mask_u8[0:1, :, :], -1.0, -MASKED, ALU.add, ALU.mult)
            dve.tensor_reduce(valid[:, :], mask_u8[:, :, :], AX.X, ALU.max)
            stats_q(1)
            split_first(1)

            def first_maxima(i, q):
                for j in range(4):
                    dve.wait_ge(s["scores_ready"], NH * i + 4 * q + j + 1)
                    dve.tensor_reduce(row_max[:, i, :, 4 * q + j],
                                      first_score_bank[j][:, :].rearrange("p (m n) -> p m n", m=2),
                                      AX.X, ALU.max).then_inc(s["max_done"], 1)

            with dve.Fori(0, NH // 4) as q:
                first_maxima(0, q)
            first_maxima(1, 0)
            neg_low(0, 0)
            first_maxima(1, 1)
            stats_q(2)
            unit(0, True, False, False, True, True)
            unit(1, False, True, False, True, True)
            with dve.Fori(2, NU - 3) as u:
                unit(u, False, False, False, True, True)
            unit(NU - 3, False, False, False, True, False)
            unit(NU - 2, False, False, False, False, False)
            unit(NU - 1, False, False, True, False, False)
            gather_parts(NB - 1, 1)
            invert(NB - 1, 1)
            bring_over(NB - 1, 1)
            add_x1(NB - 1, NU - 1, 1, False)
            take_yw(NB - 2)
            scale_rows(NB - 1, 1, False)
            take_yw(NB - 1)

            k[0] = n_consts
            dve.wait_ge(s["yw_done"], NB)
            link(dve.tensor_reduce(lg_max[:, :], logits[:, :, :], AX.X, ALU.max))
            dve.tensor_tensor(logits[:, :, :], logits[:, :, :], lg_max[:, :].unsqueeze(2).to_broadcast([P, NB, NE]),
                              ALU.subtract).then_inc(s["sh_exp"], 1)
            dve.wait_ge(s["sh_exp"], 2)
            link(dve.tensor_reduce(lg_sum[:, :], logits[:, :, :], AX.X, ALU.add))
            link(dve.reciprocal(lg_inv[:, :], lg_sum[:, :]))
            dve.tensor_tensor(logits[:, :, :], logits[:, :, :], lg_inv[:, :].unsqueeze(2).to_broadcast([P, NB, NE]),
                              ALU.mult).then_inc(s["sh_exp"], 1)
            dve.memset(thr[:, :], 0)
            dve.memset(taken[:, :], 0)
            dve.memset(trial[:, 0, :], 4 ** DIGITS)
            for n in range(3):
                dve.memset(cand[:, n:n + 1], (n + 1) * 4 ** (DIGITS - 1))
                ins = dve.memset(trial[:, 1, n:n + 1], (n + 1) * 4 ** (DIGITS - 1))
            ins.then_inc(s["cand_ready"], 1)
            dve.wait_ge(s["st_t"], 1)
            link(dve.tensor_copy(st_probs[:, :, :], t0_bank[:, 0:2 * P].rearrange("p (g t) -> p g t", g=2)))
            link(dve.tensor_copy(st_high[:, :, :], st_probs[:, :, :].bitcast(BF16)[:, :, 1:2 * P:2]))

            def find_digit(n, keys, marks):
                dve.wait_ge(s["cand_ready"], 4 * n + 1)
                for m in range(3):
                    ins = dve.tensor_scalar(marks[m][:, :, :], keys[:, :, :], cand[:, m:m + 1].bitcast(F32), None,
                                            ALU.is_ge, ALU.add, accum_out=count[:, m:m + 1])
                ins.then_inc(s["counted"], 1)
                dve.tensor_tensor(thr[:, :], thr[:, :], taken[:, :], ALU.bitwise_or)
                dve.tensor_scalar(trial[:, :, :], trial[:, :, :], 2, None, ALU.logical_shift_right).then_inc(s["cand_ready"], 1)
                dve.wait_ge(s["cand_ready"], 4 * n + 2)
                dve.wait_ge(s["totalled"], n + 1)
                dve.scalar_tensor_tensor(reached[:, :], t1_bank[:, 0:3], float(KE), trial[:, 0, :],
                                         ALU.is_ge, ALU.mult, accum_out=digit[:, :]).then_inc(s["cand_ready"], 1)
                dve.wait_ge(s["cand_ready"], 4 * n + 3)
                dve.tensor_copy(taken[:, :], digit[:, :]).then_inc(s["cand_ready"], 1)
                dve.wait_ge(s["cand_ready"], 4 * n + 4)
                dve.scalar_tensor_tensor(cand[:, :], trial[:, 1, :], thr[:, 0:1], taken[:, 0:1].to_broadcast([P, 3]),
                                         ALU.bitwise_or, ALU.bitwise_or).then_inc(s["cand_ready"], 1)

            for n in range(HIGH_DIGITS):
                find_digit(n, st_high, high_marks)
            with dve.Fori(0, (DIGITS - HIGH_DIGITS) // DIGITS_A_TURN) as turn:
                for r in range(DIGITS_A_TURN):
                    find_digit(turn * DIGITS_A_TURN + HIGH_DIGITS + r, st_probs, [junk, above, equal])
            link(dve.tensor_tensor(thr[:, :], thr[:, :], taken[:, :], ALU.bitwise_or))
            threshold = thr[:, :].bitcast(F32)
            dve.tensor_scalar(above[:, :, :], st_probs[:, :, :], threshold, None, ALU.is_gt, ALU.add,
                              accum_out=count[:, 0:1]).then_inc(s["counted"], 1)
            link(dve.tensor_scalar(equal[:, :, :], st_probs[:, :, :], threshold, None, ALU.is_equal))
            for g in range(2):
                link(dve.tensor_tensor_scan(running[:, g, :], ones[:, :], equal[:, g, :], 0.0, ALU.mult, ALU.add))
            dve.tensor_copy(totals[:, :], running[:, :, P - 1]).then_inc(s["eq_counted"], 1)
            dve.wait_ge(s["gt_total"], 1)
            dve.wait_ge(s["eq_total"], 1)
            link(dve.tensor_scalar(need[:, :], t1_bank[:, 3:4], -1.0, float(KE), ALU.mult, ALU.add))
            link(dve.tensor_copy(base[:, :], t1_bank[:, 4:6]))
            link(dve.tensor_tensor(base[:, 1:2], t1_bank[:, 6:7], base[:, 1:2], ALU.add))
            for g in range(2):
                link(dve.tensor_scalar(running[:, g, :], running[:, g, :], base[:, g:g + 1], need[:, 0:1], ALU.add, ALU.is_le))
            link(dve.tensor_tensor(equal[:, :, :], equal[:, :, :], running[:, :, :], ALU.mult))
            link(dve.tensor_tensor(above[:, :, :], above[:, :, :], equal[:, :, :], ALU.add))
            dve.tensor_tensor(gated[:, :, :], above[:, :, :], st_probs[:, :, :], ALU.mult).then_inc(s["gated_ready"], 1)
            dve.wait_ge(s["gate_t"], 1)
            link(dve.tensor_copy(gate[:, :], t0_bank[:, 0:NB]))

            def c_stats(t, first):
                for i in range(2):
                    b = 2 * t + i
                    if first:
                        dve.wait_ge(s["kept"], NB)
                    else:
                        dve.wait_ge(s["c_x3"], b - 1)
                    dve.scalar_tensor_tensor(x_new[:, i, :], y[:, b, :], gate[:, bass.ds(b, 1)], xs[:, b, :],
                                             ALU.mult, ALU.add).then_inc(s["c_bn"], 1)
                for i in range(2):
                    dve.wait_ge(s["c_bn"], 4 * t + 1 + i)
                    dve.bn_stats(st[:, i, :], x_new[:, i, :]).then_inc(s["c_bn"], 1)
                for i in range(2):
                    wait_apart(dve, s["c_bn"], 4 * t + 3 + i)
                    dve.bn_aggr(mv[:, i, :], st[:, i, :]).then_inc(s["c_stats"], 1)

            def c_scale(b, i, first):
                if not first:
                    dve.wait_ge(s["c_xn_t"], b - 1)
                dve.wait_ge(s["c_root"], b + 1)
                dve.tensor_scalar(xn[:, i, :], x_new[:, i, :], mv[:, i, 0:1], rstd[:, i:i + 1],
                                  ALU.subtract, ALU.mult).then_inc(s["c_xn"], 1)

            def d_scale(b, i, first):
                if not first:
                    dve.wait_ge(s["d_gath"], b - 1)
                dve.wait_ge(s["d_root"], b + 1)
                dve.tensor_scalar(z[:, i, :], x_new3[:, i, :], mv3[:, i, 0:1], rstd3[:, i:i + 1],
                                  ALU.subtract, ALU.mult).then_inc(s["d_z"], 1)

            def c_max(b, i):
                dve.wait_ge(s["c_scores"], b + 1)
                dve.tensor_reduce(sc_max[:, i:i + 1], c_bank[i][:, 256:384], AX.X, ALU.max).then_inc(s["c_max"], 1)
                dve.wait_ge(s["c_max"], b + 1)
                dve.tensor_scalar(sc_bias[:, i:i + 1], sc_max[:, i:i + 1], -(D ** -0.5), None,
                                  ALU.mult).then_inc(s["c_bias"], 1)

            def c_add(t, first):
                for i in range(2):
                    dve.wait_ge(s["c_exp"], 2 * t + i + 1)
                    dve.reciprocal(sc_inv[:, i:i + 1], sc_sum[:, i:i + 1]).then_inc(s["c_coef"], 1)
                for i in range(2):
                    dve.wait_ge(s["c_coef"], 4 * t + 1 + i)
                    dve.tensor_tensor(sc_coef[:, i:i + 1], sc_inv[:, i:i + 1], valid[:, bass.ds(2 * t + i, 1)],
                                      ALU.mult).then_inc(s["c_coef"], 1)
                for i in range(2):
                    b = 2 * t + i
                    dve.wait_ge(s["c_coef"], 4 * t + 3 + i)
                    dve.wait_ge(s["c_read"], b + 1)
                    if not first:
                        dve.wait_ge(s["kept"], NB + b - 1)
                    dve.scalar_tensor_tensor(x_new3[:, i, :], c_bank[i][:, 0:D], sc_coef[:, i:i + 1], x_new[:, i, :],
                                             ALU.mult, ALU.add).then_inc(s["c_x3"], 1)

            def d_stats(b, i):
                dve.wait_ge(s["c_x3"], b + 1)
                dve.bn_stats(st3[:, i, :], x_new3[:, i, :]).then_inc(s["d_bn"], 1)
                wait_apart(dve, s["d_bn"], b + 1)
                dve.bn_aggr(mv3[:, i, :], st3[:, i, :]).then_inc(s["d_stats"], 1)

            def d_score(b, i):
                dve.wait_ge(s["d_z"], b + 1)
                dve.tensor_tensor_reduce(out=z_work[:, i, :], in0=z[:, i, :], in1=wr_rows[:, :], scale=1.0, scalar=0.0,
                                         op0=ALU.mult, op1=ALU.add, accum_out=score0[:, i:i + 1]).then_inc(s["d_dot"], 1)
                dve.wait_ge(s["d_dot"], b + 1)
                dve.tensor_tensor(score[:, i:i + 1], score0[:, i:i + 1], br_rows[:, :], ALU.add).then_inc(s["d_score"], 1)

            def d_pick(t, first):
                row = [d_bank[i][:, 0:P] for i in range(2)]
                for i in range(2):
                    dve.wait_ge(s["d_row"], 2 * t + i + 1)
                    dve.tensor_scalar(cmp_work[:, i, :], row[i], score[:, i:i + 1], None, ALU.is_gt, ALU.add,
                                      accum_out=rank_gt[:, i:i + 1]).then_inc(s["d_rank"], 1)
                for i in range(2):
                    dve.wait_ge(s["d_rank"], 6 * t + 1 + i)
                    dve.scalar_tensor_tensor(cmp_work[:, i, :], row[i], score[:, i:i + 1], earlier[:, :], ALU.is_equal, ALU.mult,
                                             accum_out=rank_eq[:, i:i + 1]).then_inc(s["d_rank"], 1)
                for i in range(2):
                    dve.wait_ge(s["d_rank"], 6 * t + 3 + i)
                    dve.tensor_tensor(rank[:, i:i + 1], rank_gt[:, i:i + 1], rank_eq[:, i:i + 1], ALU.add).then_inc(s["d_rank"], 1)
                for i in range(2):
                    dve.wait_ge(s["d_rank"], 6 * t + 5 + i)
                    if not first:
                        dve.wait_ge(s["d_gath"], 2 * t + i - 1)
                        dve.wait_ge(s["d_pickbf"], 2 * t + i - 1)
                    dve.tensor_scalar(pick[:, i, :], free_f[:, 0:KT], rank[:, i:i + 1], None, ALU.is_equal).then_inc(s["d_pick"], 1)

            def f_take(t, first):
                if not first:
                    dve.wait_ge(s["f_sc"], 2 * t)
                dve.wait_ge(s["f_y"], t + 1)
                dve.tensor_tensor(taken_out[:, :], y_bank[:, 0:D], b2_rows[:, :], ALU.add).then_inc(s["f_taken"], 1)

            def f_add(b, i):
                dve.wait_ge(s["kept"], NB + b + 1)
                dve.wait_ge(s["f_sc"], b + 1)
                dve.tensor_tensor(out_rows[:, b, :], put_bank[i][:, 0:D], xs[:, b, :],
                                  ALU.add).then_inc(s["f_out"], 1)

            def turn(v, c, d, f, o, more_c):
                for i in range(2):
                    if d:
                        d_scale(2 * v - 2 + i, i, is_n(v, 1))
                for i in range(2):
                    if d:
                        d_score(2 * v - 2 + i, i)
                for i in range(2):
                    if c:
                        c_max(2 * v + i, i)
                for i in range(2):
                    if o:
                        f_add(2 * v - 6 + i, i)
                if d:
                    d_pick(v - 1, is_n(v, 1))
                if c:
                    c_add(v, is_n(v, 0))
                if more_c:
                    c_stats(v + 1, False)
                for i in range(2):
                    if c:
                        d_stats(2 * v + i, i)
                    if more_c:
                        c_scale(2 * v + 2 + i, i, False)
                if f:
                    f_take(v - 2, is_n(v, 2))

            c_stats(0, True)
            for i in range(2):
                c_scale(i, i, True)
            turn(0, True, False, False, False, True)
            turn(1, True, True, False, False, True)
            turn(2, True, True, True, False, True)
            with dve.Fori(3, NU - 1) as v:
                turn(v, True, True, True, True, True)
            turn(NU - 1, True, True, True, True, False)
            turn(NU, False, True, True, True, False)
            turn(NU + 1, False, False, True, True, False)
            turn(NU + 2, False, False, False, True, False)

        @block.scalar
        def _(act):
            def exponential(t, j, first):
                act.wait_ge(s["scorest_ready"], t + 1)
                if not first:
                    act.wait_ge(s["pv_done"], t - 3)
                act.activation(probs[:, j % 4, :], scoret_bank[j % 2][:, :], ACT.Exp).then_inc(s["exp_done"], 1)

            def neg_high(b, u, i):
                act.wait_ge(s["max_t"], b + 1)
                if not is_first(u):
                    act.wait_ge(neg_loaded[i], 32 * u)
                act.mul(neg_max[:, i, 0, :], t0_bank[0:NH, 0:D], -1.0).then_inc(s["neg_hi"], 1)

            def take_vt(u):
                act.wait_ge(s["ctx_t"], u + 1)
                act.copy(vt[:, bass.ds(2 * u, 2), :, :].rearrange("p b k c -> p (b k c)"),
                         t0_bank[:, :]).then_inc(s["vt_done"], 1)

            def high_k(u):
                if not is_first(u):
                    act.wait_ge(s["parts_written"], 96 * u)
                act.wait_ge(s["staged"], 32 * (u + 1))
                act.copy(k_parts[:, 0, :], ctx_stage[:, :, :].rearrange("p b n -> p (b n)")).then_inc(s["k_high"], 1)

            def mid_k(u):
                act.wait_ge(s["k_rest"], u + 1)
                act.copy(k_parts[:, 1, :], k_rest[:, :]).then_inc(s["k_mid"], 1)

            def high_q(u):
                act.wait_ge(s["q_ready"], u + 1)
                act.copy(q_parts[:, 0, :], qn[:, :, :].rearrange("p b n -> p (b n)")).then_inc(s["q_high"], 1)

            def mid_q(u):
                act.wait_ge(s["q_rest"], u + 1)
                act.copy(q_parts[:, 1, :], q_rest[:, :]).then_inc(s["q_mid"], 1)

            def take_even(b, i, first):
                act.wait_ge(s["pv_done"], NH * (b + 1))
                if not first:
                    act.wait_ge(s["div_step"], 5 * (b - 1))
                act.mul(sum_high[:, i, :], pv_bank[i][:, 0:D], high[:, 0:1])
                act.mul(num_low[:, i, :], pv_bank[i][:, 0:D], low[:, 0:1]).then_inc(s["even_taken"], 1)

            def take_xnt(b, i, first):
                act.wait_ge(s["xn_t"], b + 1)
                if not first:
                    act.wait_ge(s["yw_ready"], b - 1)
                act.copy(xnt[:, i].rearrange("p k t -> p (k t)"), t1_bank[:, 0:D]).then_inc(s["xnt_copied"], 1)

            high_k(0)
            mid_k(0)
            take_vt(0)
            high_q(0)
            mid_q(0)
            high_k(1)
            mid_k(1)
            take_vt(1)
            high_q(1)
            mid_q(1)
            neg_high(0, 0, 0)
            act.wait_ge(s["neg_done"], 1)
            for part in range(2):
                act.dma_start(q_stack[QROWS + part:QROWS + part + 1, 0, :, 0, :],
                              neg_max[:, 0, part, :]).then_inc(neg_loaded[0], 16)
            high_k(2)

            def unit(u, first, second, last, parts, more_parts):
                for j in range(STEPS):
                    exponential(STEPS * u + j, j, first and j < 4)
                    if j == 0 and not first:
                        take_even(2 * u - 1, 1, second)
                    if j == 0 and parts:
                        mid_k(u + 2)
                    if j == 0:
                        neg_high(2 * u + 1, u, 1)
                    if j == 2 and not first:
                        take_xnt(2 * u - 2, 0, second)
                    if j == 2 and parts:
                        high_q(u + 2)
                    if j == 4 and parts:
                        mid_q(u + 2)
                    if j == 6 and parts:
                        take_vt(u + 2)
                    if j == 8:
                        take_even(2 * u, 0, first)
                    if j == 9 and not last:
                        neg_high(2 * u + 2, u + 1, 0)
                    if j == 10 and not first:
                        take_xnt(2 * u - 1, 1, second)
                    if j == 13 and more_parts:
                        high_k(u + 3)

            unit(0, True, False, False, True, True)
            unit(1, False, True, False, True, True)
            with act.Fori(2, NU - 3) as u:
                unit(u, False, False, False, True, True)
            unit(NU - 3, False, False, False, True, False)
            unit(NU - 2, False, False, False, False, False)
            unit(NU - 1, False, False, True, False, False)
            take_even(NB - 1, 1, False)
            take_xnt(NB - 2, 0, False)
            take_xnt(NB - 1, 1, False)

            act.wait_ge(s["sh_exp"], 1)
            act.activation(logits[:, :, :], logits[:, :, :], ACT.Exp).then_inc(s["sh_exp"], 1)

            def turn(v, c, d, f):
                if c:
                    for i in range(2):
                        act.wait_ge(s["c_xn_t"], 2 * v + i + 1)
                        if not is_n(v, 0):
                            act.wait_ge(s["c_scores"], 2 * v + i - 1)
                        act.copy(xnt[:, i].rearrange("p k t -> p (k t)"), c_bank[i][:, 0:D]).then_inc(s["c_xnt"], 1)
                    for i in range(2):
                        act.wait_ge(s["c_bias"], 2 * v + i + 1)
                        if not is_n(v, 0):
                            act.wait_ge(s["c_attn_t"], 2 * v + i - 1)
                            act.wait_ge(s["c_coef"], 4 * v + 2 * i - 2)
                        act.activation(attn[:, i, :], c_bank[i][:, 256:384], ACT.Exp, bias=sc_bias[:, i:i + 1],
                                       scale=D ** -0.5, accum_out=sc_sum[:, i:i + 1]).then_inc(s["c_exp"], 1)
                    for i in range(2):
                        act.wait_ge(s["c_attn_t"], 2 * v + i + 1)
                        if not is_n(v, 0):
                            act.wait_ge(s["c_read"], 2 * v + i - 1)
                        act.copy(attn_t[:, i, :], c_bank[i][:, 384:512]).then_inc(s["c_attnt"], 1)
                if f:
                    t = v - 2
                    if not is_n(v, 2):
                        act.wait_ge(s["f_y"], t)
                    for h in range(NF):
                        act.wait_ge(s["f_h"], NF * t + (h // 4 + 1) * 4)
                        act.activation(hid[:, h, :], hid_bank[h // 4][:, (h % 4) * P:(h % 4 + 1) * P], ACT.Gelu_apprx_tanh,
                                       bias=b1s[:, h:h + 1]).then_inc(s["f_gelu"], 1)
                if d:
                    for i in range(2):
                        b = 2 * v - 2 + i
                        act.wait_ge(s["d_gath"], b + 1)
                        act.copy(zg[:, :, bass.ds(KT * b, KT)],
                                 d_bank[i][:, P:2 * P].rearrange("p (k t) -> p k t", k=2)).then_inc(s["d_zg"], 1)
                if f:
                    act.wait_ge(s["f_pt"], t + 1)
                    if not is_n(v, 2):
                        act.wait_ge(s["f_sc"], 2 * t)
                    act.copy(pick_t[:, :], pick_t_psum).then_inc(s["f_ptc"], 1)

            turn(0, True, False, False)
            turn(1, True, True, False)
            turn(2, True, True, True)
            with act.Fori(3, NU) as v:
                turn(v, True, True, True)
            turn(NU, False, True, True)
            turn(NU + 1, False, False, True)

        @block.tensor
        def _(pe):
            def scores(to, u, b_in, h, free):
                if not (isinstance(free, int) and free < 1):
                    pe.wait_ge(s["max_done"], free)
                slot = u % SLOTS
                for m in range(2):
                    ins = pe.matmul(to[:, m * D:(m + 1) * D],
                                    q_stack[0:QROWS, slot, h, b_in, m * P:(m + 1) * P],
                                    k_stack[0:QROWS, slot, h, b_in, :], start=True, stop=True)
                ins.then_inc(s["scores_ready"], 1)

            def scores_t(t, u, j, free):
                b_in, h = j // NH, j % NH
                if free:
                    pe.wait_ge(s["exp_done"], t - 1)
                if h == 0:
                    pe.wait_ge(neg_loaded[b_in], 32 * (u + 1))
                slot = u % SLOTS
                for k in range(2):
                    ins = pe.matmul(scoret_bank[j % 2][:, k * D:(k + 1) * D],
                                    k_stack[0:SROWS, slot, h, b_in, k * P:(k + 1) * P],
                                    q_stack[0:SROWS, slot, h, b_in, :], start=True, stop=True)
                ins.then_inc(s["scorest_ready"], 1)

            def values(t, b, j, first):
                i, h = j // NH, j % NH
                if h == 0:
                    pe.wait_ge(s["values_ready"], b + 1)
                    if not first:
                        pe.wait_ge(s["div_step"], 5 * (b - 2) + 2)
                pe.wait_ge(s["exp_done"], t + 1)
                pair, odd = h // 2, h % 2
                for k in range(2):
                    ins = pe.matmul(pv_bank[i][pair * Q:(pair + 1) * Q, odd * D:(odd + 1) * D],
                                    values_ones[:, i, k, pair, odd, :], probs[:, j % 4, k * D:(k + 1) * D],
                                    start=(k == 0), stop=(k == 1))
                ins.then_inc(s["pv_done"], 1)

            def max_t(b, i):
                pe.wait_ge(s["max_done"], NH * (b + 1))
                for m in range(2):
                    ins = pe.transpose(t0_bank[0:NH, m * P:(m + 1) * P], row_max[:, i, m, :], ident[:, :])
                ins.then_inc(s["max_t"], 1)

            def ctx_t(u):
                pe.wait_ge(s["staged"], 32 * (u + 1))
                for i in range(2):
                    for k in range(2):
                        ins = pe.transpose(t0_bank[:, (2 * i + k) * P:(2 * i + k + 1) * P],
                                           ctx_stage[:, i, k * P:(k + 1) * P], ident[:, :])
                ins.then_inc(s["ctx_t"], 1)

            def xn_t(b, i):
                pe.wait_ge(s["xn_ready"], b + 1)
                for k in range(2):
                    ins = pe.transpose(t1_bank[:, k * P:(k + 1) * P], xn[:, i, k * P:(k + 1) * P], ident[:, :])
                ins.then_inc(s["xn_t"], 1)

            def yw(b, i):
                pe.wait_ge(s["xnt_copied"], b + 1)
                for k in range(2):
                    ins = pe.matmul(t1_bank[:, 0:D + NE], xnt[:, i, k, :], wr_moving[:, k, :],
                                    start=(k == 0), stop=(k == 1))
                ins.then_inc(s["yw_ready"], 1)

            pe.wait_ge(s["ident_done"], 1)
            pe.wait_ge(s["ones_done"], 1)
            ctx_t(0)
            pe.wait_ge(s["vt_done"], 1)
            ctx_t(1)
            pe.wait_ge(s["stacks_loaded"], 96)
            for step in range(STEPS):
                scores(first_score_bank[step % 4], 0, step // NH, step % NH, step - 3)
                if step == NH + 3:
                    pe.wait_ge(s["vt_done"], 2)
                    max_t(0, 0)
            pe.wait_ge(s["w_ones"], 16)
            scores_t(0, 0, 0, False)
            scores_t(1, 0, 1, False)

            def unit(u, first, second, last, parts):
                for j in range(STEPS):
                    if not last:
                        if j == 0:
                            pe.wait_ge(s["stacks_loaded"], 96 * (u + 2))
                        scores(score_bank[j % 2], u + 1, j // NH, j % NH, STEPS * (u + 1) + j - 1)
                    if j < STEPS - 2:
                        scores_t(STEPS * u + j + 2, u, j + 2, True)
                    elif not last:
                        scores_t(STEPS * (u + 1) + j - 14, u + 1, j - 14, True)
                    if j == 0:
                        pe.wait_ge(s["neg_done"], 2 * u + 1)
                        max_t(2 * u + 1, 1)
                    if j == 8 and not last:
                        if parts:
                            pe.wait_ge(s["vt_done"], u + 3)
                        else:
                            pe.wait_ge(s["neg_done"], 2 * u + 2)
                        max_t(2 * u + 2, 0)
                    values(STEPS * u + j, 2 * u + j // NH, j, first)
                    if j == 0 and not first:
                        if not second:
                            pe.wait_ge(s["yw_done"], 2 * u - 2)
                        xn_t(2 * u - 2, 0)
                    if j == 5 and not first:
                        if second:
                            pe.wait_ge(s["w_small"], 16 * 9)
                        yw(2 * u - 2, 0)
                    if j == 4 and parts:
                        pe.wait_ge(s["neg_done"], 2 * u + 2)
                        ctx_t(u + 2)
                    if j == 8 and not first:
                        pe.wait_ge(s["yw_done"], 2 * u - 1)
                        xn_t(2 * u - 1, 1)
                    if j == 11 and not first:
                        yw(2 * u - 1, 1)

            unit(0, True, False, False, True)
            unit(1, False, True, False, True)
            with pe.Fori(2, NU - 2) as u:
                unit(u, False, False, False, True)
            unit(NU - 2, False, False, False, False)
            unit(NU - 1, False, False, True, False)
            for i in range(2):
                b = NB - 2 + i
                pe.wait_ge(s["yw_done"], b)
                xn_t(b, i)
                yw(b, i)

            pe.wait_ge(s["sh_exp"], 3)
            for g in range(2):
                ins = pe.transpose(t0_bank[:, g * P:(g + 1) * P],
                                   logits[:, NH * g:NH * (g + 1), :].rearrange("p b e -> p (b e)"), ident[:, :])
            ins.then_inc(s["st_t"], 1)

            def total(n):
                pe.wait_ge(s["counted"], n + 1)
                pe.matmul(t1_bank[:, 0:3], same_expert[:, :], count[:, :], start=True, stop=True).then_inc(s["totalled"], 1)

            for n in range(HIGH_DIGITS):
                total(n)
            with pe.Fori(0, (DIGITS - HIGH_DIGITS) // DIGITS_A_TURN) as turn:
                for r in range(DIGITS_A_TURN):
                    total(turn * DIGITS_A_TURN + HIGH_DIGITS + r)
            pe.wait_ge(s["counted"], DIGITS + 1)
            pe.matmul(t1_bank[:, 3:4], same_expert[:, :], count[:, 0:1], start=True, stop=True).then_inc(s["gt_total"], 1)
            pe.wait_ge(s["eq_counted"], 1)
            pe.matmul(t1_bank[:, 4:6], earlier_batch[:, :], totals[:, :], start=True, stop=True)
            pe.matmul(t1_bank[:, 6:7], same_expert[:, :], totals[:, 0:1], start=True, stop=True).then_inc(s["eq_total"], 1)
            pe.wait_ge(s["gated_ready"], 1)
            for g in range(2):
                ins = pe.matmul(t0_bank[:, NH * g:NH * (g + 1)], gated[:, g, :], batch_of[:, :], start=True, stop=True)
            ins.then_inc(s["gate_t"], 1)

            def hidden(t, h):
                for k in range(2):
                    ins = pe.matmul(hid_bank[h // 4][:, (h % 4) * P:(h % 4 + 1) * P], w1s[:, k, h * P:(h + 1) * P],
                                    zg[:, k, bass.ds(P * t, P)], start=(k == 0), stop=(k == 1))
                ins.then_inc(s["f_h"], 1)

            def turn(v, c, d, f, o):
                t = v - 2
                if f:
                    if is_n(v, 2):
                        pe.wait_ge(s["w_big"], 16 * 3)
                    pe.wait_ge(s["d_zg"], 2 * t + 2)
                    if not is_n(v, 2):
                        pe.wait_ge(s["f_gelu"], NF * t)
                    for h in range(0, 2):
                        hidden(t, h)
                for i in range(2):
                    if c:
                        b = 2 * v + i
                        pe.wait_ge(s["c_xn"], b + 1)
                        if not is_n(v, 0):
                            pe.wait_ge(s["c_x3"], b - 1)
                        for k in range(2):
                            ins = pe.transpose(c_bank[i][:, k * P:(k + 1) * P], xn[:, i, k * P:(k + 1) * P], ident[:, :])
                        ins.then_inc(s["c_xn_t"], 1)
                    if f:
                        hidden(t, 2 + i)
                if c:
                    for i in range(2):
                        b = 2 * v + i
                        pe.wait_ge(s["c_xnt"], b + 1)
                        for k in range(2):
                            pe.matmul(c_bank[i][:, 256:384], xnt[:, i, k, :], vt[:, b, k, :],
                                      start=(k == 0), stop=False)
                        ins = pe.matmul(c_bank[i][:, 256:384], ones_bf[0:1, 0:P], mask_bias[:, b, :], start=False, stop=True)
                        ins.then_inc(s["c_scores"], 1)
                if o:
                    pe.wait_ge(s["f_taken"], t)
                    pe.wait_ge(s["f_ptc"], t)
                    for i in range(2):
                        pe.matmul(put_bank[i][:, 0:D], pick_t[i * KT:(i + 1) * KT, :],
                                  taken_out[i * KT:(i + 1) * KT, :], start=True, stop=True).then_inc(s["f_sc"], 1)
                if d:
                    for i in range(2):
                        b = 2 * v - 2 + i
                        pe.wait_ge(s["d_score"], b + 1)
                        if not is_n(v, 1):
                            pe.wait_ge(s["d_zg"], b - 1)
                        pe.transpose(d_bank[i][:, 0:P], score[:, i:i + 1].to_broadcast([P, P]), ident[:, :]).then_inc(s["d_row"], 1)
                if f:
                    for h in range(4, 6):
                        hidden(t, h)
                if c:
                    for i in range(2):
                        pe.wait_ge(s["c_exp"], 2 * v + i + 1)
                        pe.transpose(c_bank[i][:, 384:512], attn[:, i, :], ident[:, :]).then_inc(s["c_attn_t"], 1)
                if f:
                    for h in range(6, 8):
                        hidden(t, h)
                if c:
                    if is_n(v, 0):
                        pe.wait_ge(s["ctx_loaded"], 16)
                    for i in range(2):
                        b = 2 * v + i
                        pe.wait_ge(s["c_attnt"], b + 1)
                        pe.matmul(c_bank[i][:, 0:D], attn_t[:, i, :], ctx[:, b, :], start=True, stop=True).then_inc(s["c_read"], 1)
                if d:
                    for i in range(2):
                        b = 2 * v - 2 + i
                        pe.wait_ge(s["d_pick"], b + 1)
                        for k in range(2):
                            ins = pe.matmul(d_bank[i][:, P + k * KT:P + (k + 1) * KT], z[:, i, k * P:(k + 1) * P],
                                            pick[:, i, :], start=True, stop=True)
                        ins.then_inc(s["d_gath"], 1)
                if f:
                    pe.wait_ge(s["d_pickbf"], 2 * t + 2)
                    if not is_n(v, 2):
                        pe.wait_ge(s["f_out"], 2 * t)
                    pe.transpose(pick_t_psum, pick_bf[:, bass.ds(2 * t, 2), :].rearrange("p b k -> p (b k)"),
                                 ident_bf[:, :]).then_inc(s["f_pt"], 1)
                    if not is_n(v, 2):
                        pe.wait_ge(s["f_taken"], t)
                    for h in range(NF):
                        pe.wait_ge(s["f_gelu"], NF * t + h + 1)
                        ins = pe.matmul(y_bank[:, 0:D], hid[:, h, :], w2s[:, h, :], start=(h == 0), stop=(h == NF - 1))
                    ins.then_inc(s["f_y"], 1)

            turn(0, True, False, False, False)
            turn(1, True, True, False, False)
            turn(2, True, True, True, False)
            with pe.Fori(3, NU) as v:
                turn(v, True, True, True, True)
            turn(NU, False, True, True, True)
            turn(NU + 1, False, False, True, True)
            turn(NU + 2, False, False, False, True)


_INS = ['x', 'ctx_2048', 'mask_BxS2_bk0', 'L0_ffn_router_w', 'L0_ffn_router_b', 'L0_ffn_expert_w',
        'L0_ffn_expert_b', 'L1_ffn_w_r', 'L1_ffn_b_r', 'L1_ffn_w1', 'L1_ffn_b1', 'L1_ffn_w2', 'L1_ffn_b2']
_OUTS = [((16, 128, 256), 'float32')]


def kernel(**inputs):
    import numpy as _np
    import concourse.bacc as _bacc
    from concourse import mybir as _mybir
    from concourse.bass_utils import run_bass_kernel_spmd as _run

    nc = _bacc.Bacc("TRN2", target_bir_lowering=False, num_devices=1)
    arrays, args = {}, []
    for name in _INS:
        a = _np.ascontiguousarray(inputs[name])
        if a.ndim == 0:
            a = a.reshape(1)
        arrays[f"in_{name}_dram"] = a
        args.append(nc.dram_tensor(f"in_{name}_dram", a.shape, _mybir.dt.from_np(a.dtype), kind="ExternalInput").ap())
    for i, (shape, dtype) in enumerate(_OUTS):
        dt = _mybir.dt.from_np(_np.dtype(dtype))
        args.append(nc.dram_tensor(f"out_{i}_dram", shape, dt, kind="ExternalOutput").ap())
    build_program(nc, *args)
    r = _run(nc, [arrays], core_ids=[0])
    return r.results[0]["out_0_dram"]
```
